# Optimizing a Trainium2 kernel written in Bass

```python
import numpy as np
import jax
import jax.numpy as jnp

def _softmax(x, axis=-1):
    return jax.nn.softmax(x, axis=axis)

def _gelu(x):
    return jax.nn.gelu(x, approximate=True)

def _silu(x):
    return jax.nn.silu(x)

def _sigmoid(x):
    return jax.nn.sigmoid(x)

def _layernorm(x, axis=-1, eps=1e-05):
    m = jnp.mean(x, axis=axis, keepdims=True)
    v = jnp.var(x, axis=axis, keepdims=True)
    return (x - m) / jnp.sqrt(v + eps)

def _scatter_add(tgt, idx, src, axis=0):
    return tgt.at[idx].add(src)

def _segment_sum(src, seg, n):
    return jax.ops.segment_sum(src, seg, n)
kernel_name = 'mk_prb_d1_jaxref_r4_baf6c6'

def setup_inputs(seed: int=0):
    np.random.seed(seed)
    _w = jnp.asarray

    def _L0_attn_setup():
        import jax, jax.numpy as jnp
        import numpy as np
        HEADS = 16
        HIDDEN = 256
        key = jax.random.key(seed)
        ks = jax.random.split(key, 9)
        E, H = (256, HIDDEN)
        N, L = (4, 512)
        s = 0.02
        return {'X_embed': jax.random.normal(ks[0], (N, L, E), dtype=jnp.float32), 'Wq': jax.random.normal(ks[1], (E, H), dtype=jnp.float32) * s, 'bq': jax.random.normal(ks[2], (H,), dtype=jnp.float32) * s, 'Wk': jax.random.normal(ks[3], (E, H), dtype=jnp.float32) * s, 'bk': jax.random.normal(ks[4], (H,), dtype=jnp.float32) * s, 'Wv': jax.random.normal(ks[5], (E, H), dtype=jnp.float32) * s, 'bv': jax.random.normal(ks[6], (H,), dtype=jnp.float32) * s, 'Wo': jax.random.normal(ks[7], (H, H), dtype=jnp.float32) * s, 'bo': jax.random.normal(ks[8], (H,), dtype=jnp.float32) * s}
    _L0_attn_in = _L0_attn_setup()

    def _L0_ffn_setup():
        import jax, jax.numpy as jnp
        import numpy as np
        B, S, H, F, G = (8, 512, 256, 1024, 128)
        EPS = 1e-05

        def _dequant(q, scales, g):
            K, N = q.shape
            w = (q.astype(jnp.float32) - 128.0).reshape(K // g, g, N) * scales[:, None, :]
            return w.reshape(K, N)
        key = jax.random.key(seed)
        ks = jax.random.split(key, 8)
        x = jax.random.normal(ks[0], (B, S, H), dtype=jnp.float32)
        ln_gamma = jnp.ones((H,), jnp.float32)
        ln_beta = jnp.zeros((H,), jnp.float32)
        fc1_q = jax.random.randint(ks[1], (H, F), 0, 64, dtype=jnp.int32)
        fc2_q = jax.random.randint(ks[2], (F, H), 0, 64, dtype=jnp.int32)
        fc1_scales = jax.random.uniform(ks[3], (H // G, F), jnp.float32) * 0.02 + 0.001
        fc2_scales = jax.random.uniform(ks[4], (F // G, H), jnp.float32) * 0.02 + 0.001
        fc1_bias = jax.random.normal(ks[5], (F,), jnp.float32) * 0.02
        fc2_bias = jax.random.normal(ks[6], (H,), jnp.float32) * 0.02
        return {'x': x, 'ln_gamma': ln_gamma, 'ln_beta': ln_beta, 'fc1_q': fc1_q, 'fc1_scales': fc1_scales, 'fc1_bias': fc1_bias, 'fc2_q': fc2_q, 'fc2_scales': fc2_scales, 'fc2_bias': fc2_bias}
    _L0_ffn_in = _L0_ffn_setup()
    _d = {'L0_attn_X_embed': _L0_attn_in['X_embed'], 'L0_attn_Wq': _L0_attn_in['Wq'], 'L0_attn_bq': _L0_attn_in['bq'], 'L0_attn_Wk': _L0_attn_in['Wk'], 'L0_attn_bk': _L0_attn_in['bk'], 'L0_attn_Wv': _L0_attn_in['Wv'], 'L0_attn_bv': _L0_attn_in['bv'], 'L0_attn_Wo': _L0_attn_in['Wo'], 'L0_attn_bo': _L0_attn_in['bo'], 'L0_ffn_ln_gamma': _L0_ffn_in['ln_gamma'], 'L0_ffn_ln_beta': _L0_ffn_in['ln_beta'], 'L0_ffn_fc1_q': _L0_ffn_in['fc1_q'], 'L0_ffn_fc1_scales': _L0_ffn_in['fc1_scales'], 'L0_ffn_fc1_bias': _L0_ffn_in['fc1_bias'], 'L0_ffn_fc2_q': _L0_ffn_in['fc2_q'], 'L0_ffn_fc2_scales': _L0_ffn_in['fc2_scales'], 'L0_ffn_fc2_bias': _L0_ffn_in['fc2_bias']}
    _x0 = _d['L0_attn_X_embed']
    _d['L0_attn_X_embed'] = jax.random.normal(jax.random.fold_in(jax.random.key(seed), 1), (8, 1024, 256), dtype=_x0.dtype)
    del _x0
    return _d

def reference(L0_attn_X_embed, L0_attn_Wq, L0_attn_bq, L0_attn_Wk, L0_attn_bk, L0_attn_Wv, L0_attn_bv, L0_attn_Wo, L0_attn_bo, L0_ffn_ln_gamma, L0_ffn_ln_beta, L0_ffn_fc1_q, L0_ffn_fc1_scales, L0_ffn_fc1_bias, L0_ffn_fc2_q, L0_ffn_fc2_scales, L0_ffn_fc2_bias):

    def _L0_attn_ref(X_embed, Wq, bq, Wk, bk, Wv, bv, Wo, bo):
        import jax, jax.numpy as jnp
        import numpy as np
        HEADS = 16
        HIDDEN = 256
        N, L, _ = X_embed.shape
        H, heads = (HIDDEN, HEADS)
        dh = H // heads
        Q = X_embed @ Wq + bq
        K = X_embed @ Wk + bk
        V = X_embed @ Wv + bv
        Q = Q.reshape(N, heads, L, dh)
        K = K.reshape(N, heads, L, dh)
        V = V.reshape(N, heads, L, dh)
        scale = np.float32(1.0 / np.sqrt(H))
        Q = Q * scale
        K = K * scale
        scores = jnp.einsum('neax,nebx->neab', Q, K)
        A = jax.nn.softmax(scores, axis=2)
        Out = jnp.einsum('neab,neax->neax', A, V)
        Out = Out.reshape(N, L, H)
        return Out @ Wo + bo

    def _L0_ffn_ref(x, ln_gamma, ln_beta, fc1_q, fc1_scales, fc1_bias, fc2_q, fc2_scales, fc2_bias):
        import jax, jax.numpy as jnp
        import numpy as np
        B, S, H, F, G = (8, 512, 256, 1024, 128)
        EPS = 1e-05

        def _dequant(q, scales, g):
            K, N = q.shape
            w = (q.astype(jnp.float32) - 128.0).reshape(K // g, g, N) * scales[:, None, :]
            return w.reshape(K, N)
        residual = x
        mu = jnp.mean(x, axis=-1, keepdims=True)
        var = jnp.mean(jnp.square(x - mu), axis=-1, keepdims=True)
        h = (x - mu) * jax.lax.rsqrt(var + EPS) * ln_gamma + ln_beta
        hf = h.reshape(-1, H)
        w1 = _dequant(fc1_q, fc1_scales, G)
        y = hf @ w1 + fc1_bias
        y = jax.nn.silu(y)
        w2 = _dequant(fc2_q, fc2_scales, G)
        z = y @ w2 + fc2_bias
        return residual + 0.5 * z.reshape(residual.shape)
    x = L0_attn_X_embed
    xn = _layernorm(x, axis=-1)
    x = x + _L0_attn_ref(xn, L0_attn_Wq, L0_attn_bq, L0_attn_Wk, L0_attn_bk, L0_attn_Wv, L0_attn_bv, L0_attn_Wo, L0_attn_bo) + _L0_ffn_ref(xn, L0_ffn_ln_gamma, L0_ffn_ln_beta, L0_ffn_fc1_q, L0_ffn_fc1_scales, L0_ffn_fc1_bias, L0_ffn_fc2_q, L0_ffn_fc2_scales, L0_ffn_fc2_bias)
    return x

_drawn_inputs = setup_inputs


def setup_inputs(seed=0):
    import zlib

    import numpy as np

    out = dict(_drawn_inputs(seed))
    spreads = {'L0_ffn_ln_gamma': (1.0, 0.2), 'L0_ffn_ln_beta': (0.0, 0.1)}
    factors = {'L0_attn_Wq': 64.0,
     'L0_attn_bq': 64.0,
     'L0_attn_Wk': 64.0,
     'L0_attn_bk': 64.0,
     'L0_attn_Wv': 64.0,
     'L0_attn_bv': 64.0,
     'L0_attn_Wo': 64.0,
     'L0_attn_bo': 64.0,
     'L0_ffn_fc1_bias': 64.0,
     'L0_ffn_fc2_bias': 64.0}
    for name, (base, spread) in spreads.items():
        noise = np.random.default_rng([zlib.crc32(name.encode()), seed]).standard_normal(out[name].shape)
        drawn = base * np.exp(spread * noise) if base else spread * noise
        out[name] = jnp.asarray(drawn.astype(out[name].dtype))
    for name, factor in factors.items():
        out[name] = (out[name] * factor).astype(out[name].dtype)
    return out
```

```python
import concourse.bass as bass
from concourse import mybir
from contextlib import ExitStack


def attention_ffn_kernel(nc, x, wq, wk, wv, wo, feature_cols, fc1_bias_cols, bo, fc1_q, fc1_scales,
                         fc2_q, fc2_scales, fc2_bias, out):
    fp32 = mybir.dt.float32
    bf16 = mybir.dt.bfloat16
    i32 = mybir.dt.int32
    ALU = mybir.AluOpType
    ACT = mybir.ActivationFunctionType
    AXX = mybir.AxisListType.X

    P = 128
    ROWS, H = x.shape
    F = fc1_q.shape[1]
    TILES = ROWS // P
    DH = 16
    NJ = H // DH
    KH = H // P
    FT = F // P
    HR = 64
    HEADS = P // HR
    TOK = HR * NJ
    KB = TOK // P
    SLOTS = HEADS * KB
    NSC = 3
    NE = 8
    LAG = 4
    QT = TOK // 4
    JQ = QT // HR
    SC = float(H) ** -0.5
    EPS = 1e-5
    Q_PARTS = (0, 0, 0, 1, 1, 2)
    K_PARTS = (0, 1, 2, 0, 1, 0)
    NP = len(Q_PARTS)
    STACK = NP * DH

    ctx = ExitStack()
    with ctx:
        def sb(name, shape, dt=fp32):
            return ctx.enter_context(nc.sbuf_tensor(name, shape, dt))

        def sem(name):
            return ctx.enter_context(nc.semaphore(name))

        identity = sb("identity", [P, P])
        wq_sb = sb("wq_sb", [P, KH, H])
        wk_sb = sb("wk_sb", [P, KH, H])
        wv_sb = sb("wv_sb", [P, KH, H])
        wo_sb = sb("wo_sb", [P, KH, H])
        cols = sb("cols", [P, 5, KH])
        b1 = sb("b1", [P, FT])
        bias_row = sb("bias_row", [P, H])
        b2_row = sb("b2_row", [P, H])
        q1 = sb("q1", [P, KH, F], i32)
        s1 = sb("s1", [P, KH, F])
        w1 = sb("w1", [P, KH, F])
        q2 = sb("q2", [P, FT, H], i32)
        s2 = sb("s2", [P, FT, H])
        w2 = sb("w2", [P, FT, H])
        xt = sb("xt", [P, 2, H])
        xn = sb("xn", [P, 2, H])
        hn = sb("hn", [P, 2, H])
        stats = sb("stats", [P, 2, 6])
        moments = sb("moments", [P, 2, 2])
        veps = sb("veps", [P, 2, 1])
        rstd = sb("rstd", [P, 2, 1])
        minus_half = sb("minus_half", [P, 1])
        residual = sb("residual", [P, 2, H])
        base = sb("base", [P, 2, H])
        xT = sb("xT", [P, 2, KH, P])
        hT = sb("hT", [P, 2, KH, P])
        qk32 = sb("qk32", [P, 2, 2 * KH, P])
        rest = sb("rest", [P, 2 * KH, P])
        parts = sb("parts", [P, 2, 2 * KH, 3, P], bf16)
        qs = sb("qs", [STACK, 2, NJ, P], bf16)
        k_in = sb("k_in", [STACK, 2, NJ, P], bf16)
        ks = sb("ks", [STACK, 2, HEADS, NJ, HR], bf16)
        nmax = sb("nmax", [P, NE, 1])
        zsum = sb("zsum", [P, NE, 1])
        rz = sb("rz", [P, NE, 32])
        ex = sb("ex", [P, NE, TOK])
        wrow = sb("wrow", [P, 2, QT])
        vT = sb("vT", [P, 2, KH, P])
        wT = sb("wT", [P, 2, KH, P])
        oT = sb("oT", [P, 2, KH, P])
        u = sb("u", [P, 2, FT, P])
        th = sb("th", [P, 2, FT, P])
        yT = sb("yT", [P, 2, FT, P])
        res = sb("res", [P, 2, H])

        score = [ctx.enter_context(nc.psum_tensor(f"score{b}", [P, TOK], fp32)) for b in range(NSC)]
        wacc = ctx.enter_context(nc.psum_tensor("wacc", [P, 512], fp32))
        dense = ctx.enter_context(nc.psum_tensor("dense", [P, 512], fp32))

        parts_d = nc.dram_tensor("parts_d", [2, 2 * KH, P, 3, P], bf16, kind="Internal").ap()
        w_d = nc.dram_tensor("w_d", [2, NJ, P], fp32, kind="Internal").ap()

        weights_in = sem("weights_in")
        cols_in = sem("cols_in")
        fc_in = sem("fc_in")
        consts_ready = sem("consts_ready")
        identity_zeroed = sem("identity_zeroed")
        setup_step = sem("setup_step")
        qkw_ready = sem("qkw_ready")
        fcw_ready = sem("fcw_ready")
        bias_ready = sem("bias_ready")
        x_loaded = [sem(f"x_loaded{k}") for k in range(2)]
        norm_step = sem("norm_step")
        rstd_ready = sem("rstd_ready")
        residual_ready = sem("residual_ready")
        base_ready = sem("base_ready")
        transposed = sem("transposed")
        xT_copied = sem("xT_copied")
        qk_ready = sem("qk_ready")
        qk_biased = sem("qk_biased")
        split_step = sem("split_step")
        parts_stored = sem("parts_stored")
        q_stacked = [sem(f"q_stacked{k}") for k in range(2)]
        k_stacked = [sem(f"k_stacked{k}") for k in range(2)]
        k_ordered = sem("k_ordered")
        scores_ready = sem("scores_ready")
        max_ready = sem("max_ready")
        exp_done = sem("exp_done")
        rz_ready = sem("rz_ready")
        wsum_done = sem("wsum_done")
        w_copied = sem("w_copied")
        w_stored = [sem(f"w_stored{k}") for k in range(2)]
        w_spread = [sem(f"w_spread{k}") for k in range(2)]
        v_ready = sem("v_ready")
        v_biased = sem("v_biased")
        oT_ready = sem("oT_ready")
        fc1_ready = sem("fc1_ready")
        u_ready = sem("u_ready")
        tanh_ready = sem("tanh_ready")
        y_step = sem("y_step")
        out_ready = sem("out_ready")
        out_added = sem("out_added")
        out_stored = [sem(f"out_stored{k}") for k in range(2)]

        block = ctx.enter_context(nc.Block())

        def within(t, lo=0, hi=TILES - 1):
            return not isinstance(t, int) or lo <= t <= hi

        def steps(engine, body, loop_end):
            for i in range(-2, LOOP_START):
                body(i, i % 2)
            with engine.Fori(LOOP_START, loop_end, 2) as i:
                body(i, 0)
                body(i + 1, 1)
            for i in range(loop_end, TILES + 1):
                body(i, i % 2)

        def wait(engine, sem_, value):
            if not isinstance(value, int) or value > 0:
                engine.wait_ge(sem_, value)

        def dma_count(t, par, dmas=1):
            return 8 * dmas * (t - par + 2)

        def wait_all(engine, *waits):
            waits = [(sem_, v) for sem_, v in waits if not isinstance(v, int) or v > 0]
            waits = [(sem_, v if isinstance(v, int) else engine.to_reg(v)) for sem_, v in waits]
            for sem_, v in waits:
                engine.wait_ge(sem_, v)

        def wait_apart(engine, *waits):
            wait_all(engine, (consts_ready, 1), *waits)

        def score_buf(par, s):
            return (SLOTS * par + s) % NSC

        def score_gap(par, s):
            n = SLOTS * par + s
            return NSC if n >= NSC or (2 * SLOTS) % NSC == 0 else (2 * SLOTS) % NSC

        def ebuf(s):
            return s % NE

        LOOP_START = 4
        LOOP_END = TILES - 4
        NORM_SLOTS = (1, 2, 3, 6, 7, 8, 9, 12)

        @block.sync
        def _(sp):
            def load_x(t, par):
                row = t * P if isinstance(t, int) else sp.snap(t * P)
                wait(sp, residual_ready, t - 1)
                sp.dma_start(xt[:, par, :], x[bass.ds(row, P), :]).then_inc(x_loaded[par], 16)

            load_x(0, 0)
            sp.dma_start(wq_sb[:], wq.rearrange("(k p) n -> p k n", p=P)).then_inc(weights_in, 16)
            sp.dma_start(wk_sb[:], wk.rearrange("(k p) n -> p k n", p=P)).then_inc(weights_in, 16)
            sp.dma_start(cols[:], feature_cols.rearrange("p (c k) -> p c k", k=KH)).then_inc(cols_in, 16)
            load_x(1, 1)
            sp.dma_start(b1[:], fc1_bias_cols).then_inc(cols_in, 16)
            sp.dma_start(bias_row[:], bo.partition_broadcast(P)).then_inc(cols_in, 16)
            sp.dma_start(b2_row[:], fc2_bias.partition_broadcast(P)).then_inc(cols_in, 16)
            sp.dma_start(wv_sb[:], wv.rearrange("(k p) n -> p k n", p=P)).then_inc(weights_in, 16)
            sp.dma_start(wo_sb[:], wo.rearrange("(k p) n -> p k n", p=P)).then_inc(weights_in, 16)
            sp.dma_start(q1[:], fc1_q.rearrange("(k p) n -> p k n", p=P)).then_inc(fc_in, 16)
            sp.dma_start(s1[:], fc1_scales.partition_broadcast(P)).then_inc(fc_in, 16)
            sp.dma_start(q2[:], fc2_q.rearrange("(k p) n -> p k n", p=P)).then_inc(fc_in, 16)
            sp.dma_start(s2[:], fc2_scales.partition_broadcast(P)).then_inc(fc_in, 16)

            def store_w(t, par, head):
                h = HEADS * t + head
                wait_all(sp, (w_copied, h + 1), (w_spread[par], dma_count(t - 2, par, KH)))
                sp.dma_start(w_d[par, :, head * HR:(head + 1) * HR].rearrange("(c j) r -> c j r", c=4),
                             wrow[0:97:32, head, :].rearrange("c (j r) -> c j r", j=JQ)).then_inc(w_stored[head], 16)

            def step(i, par):
                if within(i, -2) and within(i + 3):
                    load_x(i + 3, (par + 1) % 2)
                o = i - 1
                if within(o):
                    opar = (par + 1) % 2
                    store_w(o, opar, 1)
                    wait_all(sp, (w_stored[0], 16 * (o + 1)), (w_stored[1], 16 * (o + 1)), (oT_ready, o - 1))
                    for k in range(KH):
                        src = w_d[opar, 8 * k:8 * k + 8, :].unsqueeze(1).to_broadcast([8, DH, P])
                        sp.dma_start(wT[:, opar, k, :], src).then_inc(w_spread[opar], 16)
                n = i + 1
                if within(n):
                    npar = (par + 1) % 2
                    wait_all(sp, (split_step, 4 * (n + 1)), (q_stacked[npar], dma_count(n - 2, npar, NP)),
                             (k_stacked[npar], dma_count(n - 2, npar, NP)))
                    sp.dma_start(parts_d[npar].rearrange("b p a r -> p b (a r)"),
                                 parts[:, npar].rearrange("p b a r -> p b (a r)")).then_inc(parts_stored, 16)
                    wait_all(sp, (parts_stored, 16 * (n + 1)), (scores_ready, SLOTS * (n - 1)), (k_ordered, n - 1))
                    for dst, which, order, done in ((k_in, 1, K_PARTS, k_stacked), (qs, 0, Q_PARTS, q_stacked)):
                        for c, part in enumerate(order):
                            src = parts_d[npar, KH * which:KH * (which + 1)].rearrange("k p a r -> (k p) a r")
                            sp.dma_start(dst[DH * c:DH * (c + 1), npar],
                                         src.rearrange("(j c) a r -> c j a r", c=DH)[:, :, part]).then_inc(done[npar], 16)
                if within(i):
                    store_w(i, par, 0)
                if within(o):
                    row = o * P if isinstance(o, int) else sp.snap(o * P)
                    sp.wait_ge(out_added, o + 1)
                    sp.dma_start(out[bass.ds(row, P), :], res[:, opar, :]).then_inc(out_stored[opar], 16)

            for i in range(-1, LOOP_START):
                step(i, i % 2)
            with sp.Fori(LOOP_START, LOOP_END, 2) as i:
                step(i, 0)
                step(i + 1, 1)
            for i in range(LOOP_END, TILES + 1):
                step(i, i % 2)
            for par in range(2):
                sp.wait_ge(out_stored[par], dma_count(TILES - 2 + par, par))

        @block.gpsimd
        def _(pool):
            nc.gpsimd.memset(identity[:], 0.0).then_inc(identity_zeroed, 1)
            pool.wait_ge(identity_zeroed, 1)
            nc.gpsimd.affine_select(out=identity[:], in_=identity[:], compare_op=ALU.not_equal, fill=1.0,
                                    base=0, pattern=[[-1, P]], channel_multiplier=1).then_inc(consts_ready, 1)
            nc.gpsimd.memset(rz[:], 0.0).then_inc(consts_ready, 1)
            nc.gpsimd.memset(minus_half[:], -0.5).then_inc(identity_zeroed, 1)
            pool.wait_ge(identity_zeroed, 2)

            def rsqrt(t, which):
                pool.wait_ge(norm_step, 8 * t + 4 * which + 3)
                nc.gpsimd.tensor_tensor(rstd[:, which], veps[:, which], minus_half[:], ALU.pow).then_inc(rstd_ready, 1)

            def step(i, par):
                l, n, m, o = i + 2, i + 1, i, i - 1
                if within(m):
                    if isinstance(m, int) and m == 0:
                        pool.wait_ge(bias_ready, 1)
                    pool.wait_ge(residual_ready, m + 1)
                    wait(pool, out_added, m - 1)
                    nc.gpsimd.tensor_tensor(base[:, par], residual[:, par], bias_row[:], ALU.add).then_inc(base_ready, 1)
                if within(l):
                    rsqrt(l, 0)
                if within(n):
                    np_ = (par + 1) % 2
                    part = [parts[:, np_, :, k] for k in range(3)]
                    wait_apart(pool, (qk_biased, n + 1), (parts_stored, 16 * (n - 1)))
                    nc.gpsimd.tensor_copy(part[0], qk32[:, np_]).then_inc(split_step, 1)
                    pool.wait_ge(split_step, 4 * n + 1)
                    nc.gpsimd.tensor_tensor(rest[:], qk32[:, np_], part[0], ALU.subtract).then_inc(split_step, 1)
                    wait_apart(pool, (split_step, 4 * n + 2))
                    nc.gpsimd.tensor_copy(part[1], rest[:]).then_inc(split_step, 1)
                    pool.wait_ge(split_step, 4 * n + 3)
                    nc.gpsimd.tensor_tensor(part[2], rest[:], part[1], ALU.subtract).then_inc(split_step, 1)
                if within(l):
                    pool.wait_ge(norm_step, 8 * l + 4)
                    wait(pool, base_ready, l - 1)
                    nc.gpsimd.tensor_tensor(residual[:, par], xt[:, par], xn[:, par],
                                            ALU.add).then_inc(residual_ready, 1)
                    rsqrt(l, 1)
                if within(o):
                    op = (par + 1) % 2
                    pool.wait_ge(w_spread[op], dma_count(o, op, KH))
                    pool.wait_ge(v_biased, 2 * (o + 1))
                    wait(pool, out_ready, o - 1)
                    nc.gpsimd.tensor_tensor(oT[:, op], vT[:, op], wT[:, op], ALU.mult).then_inc(oT_ready, 1)
                if within(m):
                    for half in range(2):
                        f = slice(half * FT // 2, (half + 1) * FT // 2)
                        pool.wait_ge(tanh_ready, 2 * m + half + 1)
                        nc.gpsimd.tensor_tensor(th[:, par, f], th[:, par, f], u[:, par, f],
                                                ALU.mult).then_inc(y_step, 1)
                        pool.wait_ge(y_step, 4 * m + 2 * half + 1)
                        wait(pool, out_ready, m - 1)
                        nc.gpsimd.tensor_tensor(yT[:, par, f], th[:, par, f], u[:, par, f],
                                                ALU.add).then_inc(y_step, 1)
                if within(n):
                    wait_apart(pool, (k_stacked[np_], dma_count(n, np_, NP)), (scores_ready, SLOTS * (n - 1)))
                    nc.gpsimd.tensor_copy(ks[:, np_].bitcast(i32),
                                          k_in[:, np_].bitcast(i32).rearrange("c j (h r) -> c h j r", h=HEADS)
                                          ).then_inc(k_ordered, 1)

            steps(pool, step, LOOP_END + 2)

        @block.scalar
        def _(act):
            act.wait_ge(cols_in, 64)

            def copy_w(t, head):
                h = HEADS * t + head
                act.wait_ge(wsum_done, KB * (h + 1))
                wait(act, w_stored[head], 16 * t)
                nc.scalar.activation(wrow[:, head], wacc[:, 0:QT], ACT.Copy).then_inc(w_copied, 1)

            def step(i, par):
                l, n, m, o = i + 2, i + 1, i, i - 1
                np_ = (par + 1) % 2
                for s in range(SLOTS if within(m) else 1):
                    if within(m):
                        g = SLOTS * i + s
                        act.wait_ge(max_ready, g + 1)
                        wait(act, wsum_done, g - NE + 1)
                        nc.scalar.activation(ex[:, ebuf(s)], score[score_buf(par, s)][:], ACT.Exp,
                                             bias=nmax[:, ebuf(s)], accum_out=zsum[:, ebuf(s)]).then_inc(exp_done, 1)
                    at = (lambda k: s == k) if within(m) else (lambda k: s == 0)
                    if at(1) and within(n):
                        act.wait_ge(transposed, n + 1)
                        nc.scalar.activation(xT[:, np_], dense[:, 0:KH * P].rearrange("p (k r) -> p k r", k=KH),
                                             ACT.Copy).then_inc(xT_copied, 1)
                        for k in range(KH):
                            nc.scalar.activation(hT[:, np_, k], dense[:, (KH + k) * P:(KH + k + 1) * P], ACT.Identity,
                                                 bias=cols[:, 4, k:k + 1], scale=cols[:, 3, k:k + 1]).then_inc(xT_copied, 1)
                    if at(3) and within(o):
                        copy_w(o, 1)
                    if within(m):
                        if s == 6:
                            act.wait_ge(v_ready, m + 1)
                            wait(act, oT_ready, m - 1)
                            for k in range(KH):
                                nc.scalar.activation(vT[:, par, k], dense[:, k * P:(k + 1) * P], ACT.Identity,
                                                     bias=cols[:, 2, k:k + 1]).then_inc(v_biased, 1)
                        if s in (9, 12):
                            half = int(s == 12)
                            f = slice(half * FT // 2, (half + 1) * FT // 2)
                            act.wait_ge(u_ready, 2 * m + half + 1)
                            wait(act, y_step, 4 * (m - 2) + 2 * half + 2)
                            nc.scalar.activation(th[:, par, f], u[:, par, f], ACT.Tanh,
                                                 scale=0.5).then_inc(tanh_ready, 1)
                        if s == 11:
                            copy_w(m, 0)

            steps(act, step, LOOP_END + 2)

        @block.vector
        def _(dve):
            def chain(ins, count):
                ins.then_inc(setup_step, 1)
                dve.wait_ge(setup_step, count)

            def scale_qk():
                dve.wait_ge(weights_in, 64)
                dve.wait_ge(cols_in, 64)
                nc.vector.tensor_scalar(wq_sb[:], wq_sb[:], SC, None, ALU.mult).then_inc(qkw_ready, 1)
                nc.vector.tensor_scalar(wk_sb[:], wk_sb[:], SC, None, ALU.mult).then_inc(qkw_ready, 1)
                nc.vector.tensor_scalar(cols[:, 0:2], cols[:, 0:2], SC, None, ALU.mult).then_inc(qkw_ready, 1)
                nc.vector.scalar_tensor_tensor(bias_row[:], b2_row[:], 0.5, bias_row[:], ALU.mult,
                                               ALU.add).then_inc(bias_ready, 1)

            def dequantise():
                dve.wait_ge(fc_in, 64)
                nc.vector.scalar_tensor_tensor(w1[:], q1[:], -128.0, s1[:], ALU.add, ALU.mult).then_inc(fcw_ready, 1)
                chain(nc.vector.tensor_scalar(s2[:], s2[:], 0.25, None, ALU.mult), 1)
                nc.vector.scalar_tensor_tensor(w2[:], q2[:], -128.0, s2[:], ALU.add, ALU.mult).then_inc(fcw_ready, 1)

            def norm(t, par, k):
                if k == 0:
                    dve.wait_ge(x_loaded[par], dma_count(t, par))
                else:
                    (wait_apart if k % 4 == 1 else wait_all)(dve, (norm_step, 8 * t + k))
                src, dst = ((xt, xn), (xn, hn))[k // 4]
                which = k // 4
                if k % 4 == 0:
                    ins = nc.vector.bn_stats(stats[:, which], src[:, par])
                elif k % 4 == 1:
                    ins = nc.vector.bn_aggr(moments[:, which], stats[:, which])
                elif k % 4 == 2:
                    ins = nc.vector.tensor_scalar(veps[:, which], moments[:, which, 1:2], EPS, None, ALU.add)
                else:
                    dve.wait_ge(rstd_ready, 2 * t + which + 1)
                    wait(dve, transposed, t - 1)
                    if which == 0:
                        wait(dve, residual_ready, t - 1)
                    ins = nc.vector.tensor_scalar(dst[:, par], src[:, par], moments[:, which, 0:1], rstd[:, which],
                                                  ALU.subtract, ALU.mult)
                ins.then_inc(norm_step, 1)

            def reciprocal(g, s):
                dve.wait_ge(exp_done, g + 1)
                if isinstance(g, int) and g == 0:
                    dve.wait_ge(consts_ready, 2)
                nc.vector.reciprocal(rz[:, ebuf(s), 0:1], zsum[:, ebuf(s)]).then_inc(rz_ready, 1)

            def step(i, par):
                l, n, m, o = i + 2, i + 1, i, i - 1
                np_ = (par + 1) % 2
                if isinstance(i, int) and i == -1:
                    scale_qk()
                if isinstance(i, int) and i == 0:
                    dequantise()
                for s in range(SLOTS):
                    if within(m):
                        g = SLOTS * i + s
                        dve.wait_ge(scores_ready, g + 1)
                        nc.vector.tensor_reduce(nmax[:, ebuf(s)], score[score_buf(par, s)][:], AXX, ALU.max,
                                                negate=True).then_inc(max_ready, 1)
                    if within(SLOTS * i + s - 2, 0, SLOTS * TILES - 1):
                        reciprocal(SLOTS * i + s - 2, (s - 2) % SLOTS)
                    if s in NORM_SLOTS and within(l):
                        norm(l, par, NORM_SLOTS.index(s))
                    if s == 5 and within(n):
                        dve.wait_ge(qk_ready, n + 1)
                        wait(dve, split_step, 4 * (n - 1))
                        bias = cols[:, 0:2].rearrange("p a k -> p (a k)").unsqueeze(2).to_broadcast([P, 2 * KH, P])
                        nc.vector.tensor_tensor(qk32[:, np_], dense[:].rearrange("p (k r) -> p k r", k=2 * KH), bias,
                                                ALU.add).then_inc(qk_biased, 1)
                    if s in (8, 11) and within(m):
                        half = int(s == 11)
                        f = slice(half * FT // 2, (half + 1) * FT // 2)
                        dve.wait_ge(fc1_ready, 2 * m + half + 1)
                        wait(dve, y_step, 4 * (m - 2) + 2 * half + 2)
                        nc.vector.tensor_tensor(u[:, par, f], dense[:].rearrange("p (k r) -> p k r", k=FT // 2),
                                                b1[:, f].unsqueeze(2).to_broadcast([P, FT // 2, P]),
                                                ALU.add).then_inc(u_ready, 1)
                    if s == 15 and within(o):
                        dve.wait_ge(out_ready, o + 1)
                        dve.wait_ge(base_ready, o + 1)
                        wait(dve, out_stored[np_], dma_count(o - 2, np_))
                        nc.vector.tensor_tensor(res[:, np_], dense[:, 0:H], base[:, np_], ALU.add).then_inc(out_added, 1)

            steps(dve, step, LOOP_END + 2)

        @block.tensor
        def _(pe):
            pe.wait_ge(consts_ready, 2)

            def scores(i, par, s):
                g = SLOTS * i + s
                head, b = divmod(s, KB)
                if s == 0:
                    pe.wait_ge(q_stacked[par], dma_count(i, par, NP))
                    pe.wait_ge(k_ordered, i + 1)
                wait(pe, exp_done, g - score_gap(par, s) + 1)
                r = slice(head * HR, (head + 1) * HR)
                for a in range(2):
                    last = nc.tensor.matmul(score[score_buf(par, s)][:, 512 * a:512 * (a + 1)],
                                            ks[:, par, head, 2 * b:2 * b + 2].rearrange("c j r -> c (j r)"),
                                            qs[:, par, 8 * a:8 * a + 8, r],
                                            start=True, stop=True)
                last.then_inc(scores_ready, 1)

            def weighted_sum(i, s):
                g = SLOTS * i + s
                head, b = divmod(s, KB)
                pe.wait_ge(rz_ready, g + 1)
                if b == 0:
                    wait(pe, w_copied, HEADS * i + head)
                for c in range(4):
                    last = nc.tensor.matmul(wacc[32 * c:32 * c + 32, 0:QT], rz[:, ebuf(s)],
                                            ex[:, ebuf(s), QT * c:QT * (c + 1)],
                                            start=(b == 0), stop=(b == KB - 1), tile_position=(0, 32 * c))
                last.then_inc(wsum_done, 1)

            def project(dst, w, k0, src, last_sem=None):
                for k in range(KH):
                    last = nc.tensor.matmul(dst, w[:, k, k0:k0 + P], src[:, k], start=(k == 0), stop=(k == KH - 1))
                if last_sem is not None:
                    last.then_inc(last_sem, 1)

            def step(i, par):
                l, n, m, o = i + 2, i + 1, i, i - 1
                np_ = (par + 1) % 2
                if isinstance(i, int) and i == -1:
                    pe.wait_ge(weights_in, 64)
                    pe.wait_ge(qkw_ready, 3)
                if isinstance(i, int) and i == 0:
                    pe.wait_ge(fcw_ready, 2)
                for s in range(SLOTS):
                    if within(m):
                        scores(i, par, s)
                    if s >= LAG:
                        if within(m):
                            weighted_sum(i, s - LAG)
                    elif within(o):
                        weighted_sum(i - 1, s - LAG + SLOTS)
                    if s == 1 and within(n):
                        pe.wait_ge(norm_step, 8 * (n + 1))
                        wait(pe, out_added, n - 2)
                        for k, (src, c) in enumerate(((xn, 0), (xn, 1), (hn, 0), (hn, 1))):
                            last = nc.tensor.transpose(dense[:, P * k:P * (k + 1)], src[:, np_, P * c:P * (c + 1)],
                                                       identity[:])
                        last.then_inc(transposed, 1)
                    if s in (3, 4) and within(n):
                        if s == 3:
                            pe.wait_ge(xT_copied, 3 * (n + 1))
                        w = (wq_sb, wk_sb)[s - 3]
                        for k in range(KH):
                            q = KH * (s - 3) + k
                            project(dense[:, P * q:P * (q + 1)], w, P * k, xT[:, np_],
                                    qk_ready if q == 2 * KH - 1 else None)
                    if s == 6 and within(m):
                        if within(n):
                            pe.wait_ge(qk_biased, n + 1)
                        else:
                            pe.wait_ge(out_added, m - 1)
                        for k in range(KH):
                            project(dense[:, P * k:P * (k + 1)], wv_sb, P * k, xT[:, par],
                                    v_ready if k == KH - 1 else None)
                    if s in (7, 8, 9, 10) and within(m):
                        if s == 7:
                            pe.wait_ge(v_biased, 2 * (m + 1))
                        if s == 9:
                            pe.wait_ge(u_ready, 2 * m + 1)
                        for q in range(2):
                            f = 2 * (s - 7) + q
                            project(dense[:, P * (f % 4):P * (f % 4 + 1)], w1, P * f, hT[:, par],
                                    fc1_ready if f % 4 == 3 else None)
                    if 11 <= s <= 14 and within(o):
                        if s == 11:
                            if within(m):
                                pe.wait_ge(u_ready, 2 * m + 2)
                            else:
                                pe.wait_ge(out_added, o)
                            pe.wait_ge(y_step, 4 * (o + 1))
                        todo = {11: (0, 1, 2), 12: (3, 4, 5), 13: (6, 7), 14: (8, 9)}[s]
                        for k in todo:
                            if k == 8:
                                pe.wait_ge(oT_ready, o + 1)
                            lhs, rhs = (yT[:, np_, k], w2[:, k]) if k < FT else (oT[:, np_, k - FT], wo_sb[:, k - FT])
                            last = nc.tensor.matmul(dense[:, 0:H], lhs, rhs, start=(k == 0), stop=(k == FT + KH - 1))
                        if s == 14:
                            last.then_inc(out_ready, 1)

            steps(pe, step, LOOP_END + 2)


def kernel(**inputs):
    import numpy as np
    import concourse.bacc as bacc
    from concourse.bass_utils import run_bass_kernel_spmd

    P = 128
    a = {k.replace("L0_", ""): np.ascontiguousarray(v) for k, v in inputs.items()}
    shape = a["attn_X_embed"].shape
    rows, hidden = shape[0] * shape[1], shape[2]

    def by_feature(v):
        return v.reshape(-1, P).T

    arrays = {
        "x": a["attn_X_embed"].reshape(rows, hidden),
        "wq": a["attn_Wq"], "wk": a["attn_Wk"], "wv": a["attn_Wv"], "wo": a["attn_Wo"],
        "feature_cols": np.ascontiguousarray(np.concatenate(
            [by_feature(a[k]) for k in ("attn_bq", "attn_bk", "attn_bv", "ffn_ln_gamma", "ffn_ln_beta")], axis=1)),
        "fc1_bias_cols": np.ascontiguousarray(by_feature(a["ffn_fc1_bias"])),
        "bo": a["attn_bo"],
        "fc1_q": a["ffn_fc1_q"], "fc1_scales": a["ffn_fc1_scales"],
        "fc2_q": a["ffn_fc2_q"], "fc2_scales": a["ffn_fc2_scales"],
        "fc2_bias": a["ffn_fc2_bias"],
    }
    nc = bacc.Bacc("TRN2", target_bir_lowering=False, num_devices=1)
    args = {k: nc.dram_tensor(f"in_{k}", v.shape, mybir.dt.from_np(v.dtype), kind="ExternalInput").ap()
            for k, v in arrays.items()}
    out = nc.dram_tensor("out", (rows, hidden), mybir.dt.float32, kind="ExternalOutput").ap()
    attention_ffn_kernel(nc, **args, out=out)
    r = run_bass_kernel_spmd(nc, [{f"in_{k}": v for k, v in arrays.items()}], core_ids=[0])
    return r.results[0]["out"].reshape(shape)
```

```python
import concourse.bass as bass
from concourse import mybir
from contextlib import ExitStack


def attention_ffn_kernel(nc, x, wq, wk, wv, wo, feature_cols, fc1_bias_cols, bo, fc1_q, fc1_scales,
                         fc2_q, fc2_scales, fc2_bias, out):
    fp32 = mybir.dt.float32
    bf16 = mybir.dt.bfloat16
    i32 = mybir.dt.int32
    ALU = mybir.AluOpType
    ACT = mybir.ActivationFunctionType
    AXX = mybir.AxisListType.X

    P = 128
    ROWS, H = x.shape
    F = fc1_q.shape[1]
    TILES = ROWS // P
    DH = 16
    NJ = H // DH
    KH = H // P
    FT = F // P
    HR = 64
    HEADS = P // HR
    TOK = HR * NJ
    KB = TOK // P
    SLOTS = HEADS * KB
    NSC = 3
    NE = 8
    LAG = 5
    QT = TOK // 4
    JQ = QT // HR
    SC = float(H) ** -0.5
    EPS = 1e-5
    Q_PARTS = (0, 0, 0, 1, 1, 2)
    K_PARTS = (0, 1, 2, 0, 1, 0)
    NP = len(Q_PARTS)
    STACK = NP * DH

    ctx = ExitStack()
    with ctx:
        def sb(name, shape, dt=fp32):
            return ctx.enter_context(nc.sbuf_tensor(name, shape, dt))

        def sem(name):
            return ctx.enter_context(nc.semaphore(name))

        identity = sb("identity", [P, P])
        wq_sb = sb("wq_sb", [P, KH, H])
        wk_sb = sb("wk_sb", [P, KH, H])
        wv_sb = sb("wv_sb", [P, KH, H])
        wo_sb = sb("wo_sb", [P, KH, H])
        cols = sb("cols", [P, 5, KH])
        b1 = sb("b1", [P, FT])
        bo_row = sb("bo_row", [P, H])
        b2_row = sb("b2_row", [P, H])
        q1 = sb("q1", [P, KH, F], i32)
        s1 = sb("s1", [P, KH, F])
        w1 = sb("w1", [P, KH, F])
        q2 = sb("q2", [P, FT, H], i32)
        s2 = sb("s2", [P, FT, H])
        w2 = sb("w2", [P, FT, H])
        xt = sb("xt", [P, 2, H])
        xn = sb("xn", [P, 2, H])
        hn = sb("hn", [P, 2, H])
        stats = sb("stats", [P, 2, 6])
        moments = sb("moments", [P, 2, 2])
        veps = sb("veps", [P, 2, 1])
        rstd = sb("rstd", [P, 2, 1])
        minus_half = sb("minus_half", [P, 1])
        residual = sb("residual", [P, 2, H])
        base1 = sb("base1", [P, 2, H])
        base = sb("base", [P, 2, H])
        xT = sb("xT", [P, 2, KH, P])
        hT = sb("hT", [P, 2, KH, P])
        qk32 = sb("qk32", [P, 2, 2 * KH, P])
        rest = sb("rest", [P, 2, 2 * KH, P])
        parts = sb("parts", [P, 2, 2, 3, KH, P], bf16)
        qs = sb("qs", [STACK, 2, KH * HEADS, TOK // KH], bf16)
        ks = sb("ks", [STACK, 2, KH * HEADS, TOK // KH], bf16)
        nmax = sb("nmax", [P, NE, 1])
        zsum = sb("zsum", [P, NE, 1])
        rz = sb("rz", [P, NE, 32])
        ex = sb("ex", [P, NE, TOK])
        wrow = sb("wrow", [P, 2, QT])
        vT = sb("vT", [P, 2, KH, P])
        wT = sb("wT", [P, 2, KH, P])
        oT = sb("oT", [P, 2, KH, P])
        u = sb("u", [P, 2, FT, P])
        th = sb("th", [P, 2, FT, P])
        yT = sb("yT", [P, 2, FT, P])
        res = sb("res", [P, 2, H])

        score = [ctx.enter_context(nc.psum_tensor(f"score{b}", [P, TOK], fp32)) for b in range(NSC)]
        wacc = ctx.enter_context(nc.psum_tensor("wacc", [P, 512], fp32))
        dense = ctx.enter_context(nc.psum_tensor("dense", [P, 512], fp32))

        parts_d = nc.dram_tensor("parts_d", [2, 2, 3, KH * HEADS, P, HR], bf16, kind="Internal").ap()
        w_d = nc.dram_tensor("w_d", [2, NJ, P], fp32, kind="Internal").ap()

        weights_in = sem("weights_in")
        cols_in = sem("cols_in")
        fc_in = sem("fc_in")
        consts_ready = sem("consts_ready")
        identity_zeroed = sem("identity_zeroed")
        setup_step = sem("setup_step")
        qkw_ready = sem("qkw_ready")
        fcw_ready = sem("fcw_ready")
        bias_ready = sem("bias_ready")
        x_loaded = [sem(f"x_loaded{k}") for k in range(2)]
        stats_step = sem("stats_step")
        norm_step = sem("norm_step")
        residual_ready = sem("residual_ready")
        base1_ready = sem("base1_ready")
        base_ready = sem("base_ready")
        transposed = sem("transposed")
        xT_copied = sem("xT_copied")
        qk_ready = sem("qk_ready")
        qk_biased = sem("qk_biased")
        cast_step = sem("cast_step")
        split_step = sem("split_step")
        parts_stored = sem("parts_stored")
        q_stacked = [sem(f"q_stacked{k}") for k in range(2)]
        k_stacked = [sem(f"k_stacked{k}") for k in range(2)]
        scores_ready = sem("scores_ready")
        max_ready = sem("max_ready")
        exp_done = sem("exp_done")
        rz_ready = sem("rz_ready")
        wsum_done = sem("wsum_done")
        w_copied = sem("w_copied")
        w_stored = [sem(f"w_stored{k}") for k in range(2)]
        w_spread = [sem(f"w_spread{k}") for k in range(2)]
        v_ready = sem("v_ready")
        v_biased = sem("v_biased")
        oT_ready = sem("oT_ready")
        fc1_ready = sem("fc1_ready")
        u_ready = sem("u_ready")
        tanh_ready = sem("tanh_ready")
        y_step = sem("y_step")
        out_ready = sem("out_ready")
        out_added = sem("out_added")
        out_stored = [sem(f"out_stored{k}") for k in range(2)]

        block = ctx.enter_context(nc.Block())

        def within(t, lo=0, hi=TILES - 1):
            return not isinstance(t, int) or lo <= t <= hi

        def steps(engine, body):
            for i in range(-3, LOOP_START):
                body(i, i % 2)
            with engine.Fori(LOOP_START, LOOP_END - 1, 2) as i:
                body(i, 0)
                body(i + 1, 1)
            for i in range(LOOP_END, TILES + 1):
                body(i, i % 2)

        def wait(engine, sem_, value):
            if not isinstance(value, int) or value > 0:
                engine.wait_ge(sem_, value)

        def dma_count(t, par, dmas=1):
            return 8 * dmas * (t - par + 2)

        def wait_all(engine, *waits):
            waits = [(sem_, v) for sem_, v in waits if not isinstance(v, int) or v > 0]
            waits = [(sem_, v if isinstance(v, int) else engine.to_reg(v)) for sem_, v in waits]
            for sem_, v in waits:
                engine.wait_ge(sem_, v)

        def wait_apart(engine, *waits):
            wait_all(engine, (consts_ready, 1), *waits)

        def score_buf(par, s):
            return (SLOTS * par + s) % NSC

        def score_gap(par, s):
            n = SLOTS * par + s
            return NSC if n >= NSC or (2 * SLOTS) % NSC == 0 else (2 * SLOTS) % NSC

        def ebuf(s):
            return s % NE

        LOOP_START = 4
        LOOP_END = TILES - 4
        STATS_SLOTS = (1, 2, 3, 7, 9, 10)
        CAST_SLOTS = (9, 11)
        OUT_PRODUCTS = {9: (0,), 10: (1,), 11: (2, 3), 12: (4,), 13: (5, 6), 14: (7,), 15: (8, 9)}

        @block.sync
        def _(sp):
            def load_x(t, par):
                row = t * P if isinstance(t, int) else sp.snap(t * P)
                wait(sp, residual_ready, t - 1)
                sp.dma_start(xt[:, par, :], x[bass.ds(row, P), :]).then_inc(x_loaded[par], 16)

            load_x(0, 0)
            sp.dma_start(wq_sb[:], wq.rearrange("(k p) n -> p k n", p=P)).then_inc(weights_in, 16)
            sp.dma_start(wk_sb[:], wk.rearrange("(k p) n -> p k n", p=P)).then_inc(weights_in, 16)
            sp.dma_start(cols[:], feature_cols.rearrange("p (c k) -> p c k", k=KH)).then_inc(cols_in, 16)
            load_x(1, 1)
            sp.dma_start(b1[:], fc1_bias_cols).then_inc(cols_in, 16)
            sp.dma_start(bo_row[:], bo.partition_broadcast(P)).then_inc(cols_in, 16)
            sp.dma_start(b2_row[:], fc2_bias.partition_broadcast(P)).then_inc(cols_in, 16)
            sp.dma_start(wv_sb[:], wv.rearrange("(k p) n -> p k n", p=P)).then_inc(weights_in, 16)
            sp.dma_start(wo_sb[:], wo.rearrange("(k p) n -> p k n", p=P)).then_inc(weights_in, 16)
            sp.dma_start(q1[:], fc1_q.rearrange("(k p) n -> p k n", p=P)).then_inc(fc_in, 16)
            sp.dma_start(s1[:], fc1_scales.partition_broadcast(P)).then_inc(fc_in, 16)
            sp.dma_start(q2[:], fc2_q.rearrange("(k p) n -> p k n", p=P)).then_inc(fc_in, 16)
            sp.dma_start(s2[:], fc2_scales.partition_broadcast(P)).then_inc(fc_in, 16)

            def store_w(t, par, head):
                h = HEADS * t + head
                wait_all(sp, (w_copied, h + 1), (w_spread[par], dma_count(t - 2, par, KH)))
                sp.dma_start(w_d[par, :, head * HR:(head + 1) * HR].rearrange("(c j) r -> c j r", c=4),
                             wrow[0:97:32, head, :].rearrange("c (j r) -> c j r", j=JQ)).then_inc(w_stored[head], 16)

            def step(i, par):
                n, k, m, o = i + 2, i + 1, i, i - 1
                kpar = opar = (par + 1) % 2
                if within(i, -2) and within(i + 4):
                    load_x(i + 4, par)
                if within(k):
                    wait_all(sp, (parts_stored, 16 * (k + 1)), (scores_ready, SLOTS * (k - 1)))
                    for dst, which, order, done in ((ks, 1, K_PARTS, k_stacked), (qs, 0, Q_PARTS, q_stacked)):
                        for c, part in enumerate(order):
                            src = parts_d[kpar, which, part].rearrange("b (c j) r -> c b (j r)", c=DH)
                            sp.dma_start(dst[DH * c:DH * (c + 1), kpar], src).then_inc(done[kpar], 16)
                if within(o):
                    store_w(o, opar, 1)
                    wait_all(sp, (w_stored[0], 16 * (o + 1)), (w_stored[1], 16 * (o + 1)), (oT_ready, o - 1))
                    for h in range(KH):
                        src = w_d[opar, 8 * h:8 * h + 8, :].unsqueeze(1).to_broadcast([8, DH, P])
                        sp.dma_start(wT[:, opar, h, :], src).then_inc(w_spread[opar], 16)
                if within(m):
                    store_w(m, par, 0)
                if within(n):
                    wait_all(sp, (cast_step, 2 * (n + 1)), (split_step, 2 * (n + 1)), (q_stacked[par], dma_count(n - 2, par, NP)),
                             (k_stacked[par], dma_count(n - 2, par, NP)))
                    sp.dma_start(parts_d[par].rearrange("w a b p r -> p (w a b) r"),
                                 parts[:, par].rearrange("p w a k (h r) -> p (w a k h) r", h=HEADS)
                                 ).then_inc(parts_stored, 16)
                if within(o):
                    row = o * P if isinstance(o, int) else sp.snap(o * P)
                    sp.wait_ge(out_added, o + 1)
                    sp.dma_start(out[bass.ds(row, P), :], res[:, opar, :]).then_inc(out_stored[opar], 16)

            steps(sp, step)
            for par in range(2):
                sp.wait_ge(out_stored[par], dma_count(TILES - 2 + par, par))

        @block.gpsimd
        def _(pool):
            nc.gpsimd.memset(identity[:], 0.0).then_inc(identity_zeroed, 1)
            pool.wait_ge(identity_zeroed, 1)
            nc.gpsimd.affine_select(out=identity[:], in_=identity[:], compare_op=ALU.not_equal, fill=1.0,
                                    base=0, pattern=[[-1, P]], channel_multiplier=1).then_inc(consts_ready, 1)
            nc.gpsimd.memset(rz[:], 0.0).then_inc(consts_ready, 1)
            nc.gpsimd.memset(minus_half[:], -0.5).then_inc(identity_zeroed, 1)
            pool.wait_ge(identity_zeroed, 2)

            def normalise(t, par, which):
                src, dst = ((xt, xn), (xn, hn))[which]
                pool.wait_ge(stats_step, 6 * t + 3 * which + 3)
                nc.gpsimd.tensor_tensor(rstd[:, which], veps[:, which], minus_half[:], ALU.pow).then_inc(norm_step, 1)
                last_read = ((transposed, t - 1), (residual_ready, t - 1)) if which == 0 else ((transposed, t - 1),)
                for sem_, count in last_read:
                    wait(pool, sem_, count)
                nc.gpsimd.tensor_tensor(dst[:, par], src[:, par], moments[:, which, 0:1].to_broadcast([P, H]),
                                        ALU.subtract).then_inc(norm_step, 1)
                pool.wait_ge(norm_step, 6 * t + 3 * which + 2)
                nc.gpsimd.tensor_tensor(dst[:, par], dst[:, par], rstd[:, which].to_broadcast([P, H]),
                                        ALU.mult).then_inc(norm_step, 1)

            def silu(t, par, half):
                f = slice(half * FT // 2, (half + 1) * FT // 2)
                pool.wait_ge(tanh_ready, 2 * t + half + 1)
                nc.gpsimd.tensor_tensor(th[:, par, f], th[:, par, f], u[:, par, f], ALU.mult).then_inc(y_step, 1)
                pool.wait_ge(y_step, 4 * t + 2 * half + 1)
                wait(pool, out_ready, t - 1)
                nc.gpsimd.tensor_tensor(yT[:, par, f], th[:, par, f], u[:, par, f], ALU.add).then_inc(y_step, 1)

            def step(i, par):
                l, n, k, m, o = i + 3, i + 2, i + 1, i, i - 1
                par1 = (par + 1) % 2
                if within(m):
                    pool.wait_ge(base1_ready, m + 1)
                    wait(pool, out_added, m - 1)
                    nc.gpsimd.tensor_tensor(base[:, par], base1[:, par], b2_row[:], ALU.add).then_inc(base_ready, 1)
                if within(k):
                    if isinstance(k, int) and k == 0:
                        pool.wait_ge(bias_ready, 1)
                    pool.wait_ge(residual_ready, k + 1)
                    wait(pool, base_ready, k - 1)
                    nc.gpsimd.tensor_tensor(base1[:, par1], residual[:, par1], bo_row[:],
                                            ALU.add).then_inc(base1_ready, 1)
                if within(l):
                    normalise(l, par1, 0)
                if within(m):
                    silu(m, par, 0)
                if within(l):
                    pool.wait_ge(norm_step, 6 * l + 3)
                    wait(pool, base1_ready, l - 1)
                    nc.gpsimd.tensor_tensor(residual[:, par1], xt[:, par1], xn[:, par1],
                                            ALU.add).then_inc(residual_ready, 1)
                if within(m):
                    silu(m, par, 1)
                if within(o):
                    pool.wait_ge(w_spread[par1], dma_count(o, par1, KH))
                    pool.wait_ge(v_biased, 2 * (o + 1))
                    wait(pool, out_ready, o - 1)
                    nc.gpsimd.tensor_tensor(oT[:, par1], vT[:, par1], wT[:, par1], ALU.mult).then_inc(oT_ready, 1)
                if within(n):
                    q32, rem = (t.rearrange("p (w k) r -> p w k r", w=2) for t in (qk32[:, par], rest[:, par]))
                    pool.wait_ge(cast_step, 2 * n + 1)
                    nc.gpsimd.tensor_tensor(rem, q32, parts[:, par, :, 0], ALU.subtract).then_inc(split_step, 1)
                    pool.wait_ge(cast_step, 2 * n + 2)
                    wait(pool, parts_stored, 16 * (n - 1))
                    nc.gpsimd.tensor_tensor(parts[:, par, :, 2], rem, parts[:, par, :, 1],
                                            ALU.subtract).then_inc(split_step, 1)
                if within(l):
                    normalise(l, par1, 1)

            steps(pool, step)

        @block.scalar
        def _(act):
            act.wait_ge(cols_in, 64)

            def copy_w(t, head):
                h = HEADS * t + head
                act.wait_ge(wsum_done, KB * (h + 1))
                wait(act, w_stored[head], 16 * t)
                nc.scalar.activation(wrow[:, head], wacc[:, 0:QT], ACT.Copy).then_inc(w_copied, 1)

            def step(i, par):
                n, m, o = i + 2, i, i - 1
                par1 = (par + 1) % 2
                for s in range(SLOTS):
                    if s == 0 and within(m):
                        act.wait_ge(v_ready, m + 1)
                        wait(act, oT_ready, m - 1)
                        for k in range(KH):
                            nc.scalar.activation(vT[:, par, k], dense[:, k * P:(k + 1) * P], ACT.Identity,
                                                 bias=cols[:, 2, k:k + 1]).then_inc(v_biased, 1)
                    if s == 5 and within(n):
                        act.wait_ge(transposed, n + 1)
                        nc.scalar.activation(xT[:, par], dense[:, 0:KH * P].rearrange("p (k r) -> p k r", k=KH),
                                             ACT.Copy).then_inc(xT_copied, 1)
                        for k in range(KH):
                            nc.scalar.activation(hT[:, par, k], dense[:, (KH + k) * P:(KH + k + 1) * P], ACT.Identity,
                                                 bias=cols[:, 4, k:k + 1], scale=cols[:, 3, k:k + 1]).then_inc(xT_copied, 1)
                    if within(m):
                        g = SLOTS * i + s
                        act.wait_ge(max_ready, g + 1)
                        wait(act, wsum_done, g - NE + 1)
                        nc.scalar.activation(ex[:, ebuf(s)], score[score_buf(par, s)][:], ACT.Exp,
                                             bias=nmax[:, ebuf(s)], accum_out=zsum[:, ebuf(s)]).then_inc(exp_done, 1)
                    if s == LAG - 1 and within(o):
                        copy_w(o, 1)
                    if s == LAG + KB - 1 and within(m):
                        copy_w(m, 0)
                    if s in CAST_SLOTS and within(n):
                        c = CAST_SLOTS.index(s)
                        src, ready, count = ((qk32, qk_biased, n + 1), (rest, split_step, 2 * n + 1))[c]
                        act.wait_ge(ready, count)
                        wait(act, parts_stored, 16 * (n - 1))
                        nc.scalar.activation(parts[:, par, :, c], src[:, par].rearrange("p (w k) r -> p w k r", w=2),
                                             ACT.Copy).then_inc(cast_step, 1)
                    if s in (3, 6) and within(m):
                        half = int(s == 6)
                        f = slice(half * FT // 2, (half + 1) * FT // 2)
                        act.wait_ge(u_ready, 2 * m + half + 1)
                        wait(act, y_step, 4 * (m - 2) + 2 * half + 2)
                        nc.scalar.activation(th[:, par, f], u[:, par, f], ACT.Tanh,
                                             scale=0.5).then_inc(tanh_ready, 1)

            steps(act, step)

        @block.vector
        def _(dve):
            def chain(ins, count):
                ins.then_inc(setup_step, 1)
                dve.wait_ge(setup_step, count)

            def scale_qk():
                dve.wait_ge(weights_in, 64)
                dve.wait_ge(cols_in, 64)
                nc.vector.tensor_scalar(wq_sb[:], wq_sb[:], SC, None, ALU.mult).then_inc(qkw_ready, 1)
                nc.vector.tensor_scalar(wk_sb[:], wk_sb[:], SC, None, ALU.mult).then_inc(qkw_ready, 1)
                nc.vector.tensor_scalar(cols[:, 0:2], cols[:, 0:2], SC, None, ALU.mult).then_inc(qkw_ready, 1)
                nc.vector.tensor_scalar(b2_row[:], b2_row[:], 0.5, None, ALU.mult).then_inc(bias_ready, 1)

            def dequantise():
                dve.wait_ge(fc_in, 64)
                nc.vector.scalar_tensor_tensor(w1[:], q1[:], -128.0, s1[:], ALU.add, ALU.mult).then_inc(fcw_ready, 1)
                chain(nc.vector.tensor_scalar(s2[:], s2[:], 0.25, None, ALU.mult), 1)
                nc.vector.scalar_tensor_tensor(w2[:], q2[:], -128.0, s2[:], ALU.add, ALU.mult).then_inc(fcw_ready, 1)

            def statistics(t, par, k):
                which = k // 3
                if k == 0:
                    dve.wait_ge(x_loaded[par], dma_count(t, par))
                elif k == 3:
                    dve.wait_ge(norm_step, 6 * t + 3)
                else:
                    (wait_apart if k % 3 == 1 else wait_all)(dve, (stats_step, 6 * t + k))
                if k % 3 == 0:
                    ins = nc.vector.bn_stats(stats[:, which], (xt, xn)[which][:, par])
                elif k % 3 == 1:
                    ins = nc.vector.bn_aggr(moments[:, which], stats[:, which])
                else:
                    ins = nc.vector.tensor_scalar(veps[:, which], moments[:, which, 1:2], EPS, None, ALU.add)
                ins.then_inc(stats_step, 1)

            def reciprocals(g, s):
                dve.wait_ge(exp_done, g + 2)
                if isinstance(g, int) and g == 0:
                    dve.wait_ge(consts_ready, 2)
                e = ebuf(s)
                nc.vector.reciprocal(rz[:, e:e + 2, 0:1], zsum[:, e:e + 2]).then_inc(rz_ready, 1)

            def step(i, par):
                l, n, m, o = i + 3, i + 2, i, i - 1
                par1 = (par + 1) % 2
                if isinstance(i, int) and i == -2:
                    scale_qk()
                if isinstance(i, int) and i == -1:
                    dequantise()
                for s in range(SLOTS):
                    if within(m):
                        g = SLOTS * i + s
                        dve.wait_ge(scores_ready, g + 1)
                        nc.vector.tensor_reduce(nmax[:, ebuf(s)], score[score_buf(par, s)][:], AXX, ALU.max,
                                                negate=True).then_inc(max_ready, 1)
                    if s % 2 and within(SLOTS * i + s - 3, 0, SLOTS * TILES - 1):
                        reciprocals(SLOTS * i + s - 3, (s - 3) % SLOTS)
                    if s in STATS_SLOTS and within(l):
                        statistics(l, par1, STATS_SLOTS.index(s))
                    if s in (2, 4) and within(m):
                        half = s // 4
                        f = slice(half * FT // 2, (half + 1) * FT // 2)
                        dve.wait_ge(fc1_ready, 2 * m + half + 1)
                        wait(dve, y_step, 4 * (m - 2) + 2 * half + 2)
                        nc.vector.tensor_tensor(u[:, par, f], dense[:].rearrange("p (k r) -> p k r", k=FT // 2),
                                                b1[:, f].unsqueeze(2).to_broadcast([P, FT // 2, P]),
                                                ALU.add).then_inc(u_ready, 1)
                    if s == 8 and within(n):
                        dve.wait_ge(qk_ready, n + 1)
                        wait(dve, split_step, 2 * (n - 1))
                        bias = cols[:, 0:2].rearrange("p a k -> p (a k)").unsqueeze(2).to_broadcast([P, 2 * KH, P])
                        nc.vector.tensor_tensor(qk32[:, par], dense[:].rearrange("p (k r) -> p k r", k=2 * KH), bias,
                                                ALU.add).then_inc(qk_biased, 1)
                    if s == 15 and within(o):
                        dve.wait_ge(out_ready, o + 1)
                        dve.wait_ge(base_ready, o + 1)
                        wait(dve, out_stored[par1], dma_count(o - 2, par1))
                        nc.vector.tensor_tensor(res[:, par1], dense[:, 0:H], base[:, par1], ALU.add).then_inc(out_added, 1)

            steps(dve, step)

        @block.tensor
        def _(pe):
            pe.wait_ge(consts_ready, 2)

            def scores(i, par, s):
                g = SLOTS * i + s
                head, b = divmod(s, KB)
                if s == 0:
                    pe.wait_ge(q_stacked[par], dma_count(i, par, NP))
                    pe.wait_ge(k_stacked[par], dma_count(i, par, NP))
                wait(pe, exp_done, g - score_gap(par, s) + 1)
                half, key = b // (KB // KH), P * (b % (KB // KH))
                for a in range(KH):
                    last = nc.tensor.matmul(score[score_buf(par, s)][:, 512 * a:512 * (a + 1)],
                                            ks[:, par, HEADS * half + head, key:key + P], qs[:, par, HEADS * a + head],
                                            start=True, stop=True)
                last.then_inc(scores_ready, 1)

            def weighted_sum(i, s):
                g = SLOTS * i + s
                head, b = divmod(s, KB)
                if s % 2 == 0:
                    pe.wait_ge(rz_ready, (SLOTS // 2) * i + s // 2 + 1)
                if b == 0:
                    wait(pe, w_copied, HEADS * i + head)
                for c in range(4):
                    last = nc.tensor.matmul(wacc[32 * c:32 * c + 32, 0:QT], rz[:, ebuf(s)],
                                            ex[:, ebuf(s), QT * c:QT * (c + 1)],
                                            start=(b == 0), stop=(b == KB - 1), tile_position=(0, 32 * c))
                last.then_inc(wsum_done, 1)

            def project(dst, w, k0, src, last_sem=None):
                for k in range(KH):
                    last = nc.tensor.matmul(dst, w[:, k, k0:k0 + P], src[:, k], start=(k == 0), stop=(k == KH - 1))
                if last_sem is not None:
                    last.then_inc(last_sem, 1)

            def step(i, par):
                n, m, o = i + 2, i, i - 1
                par1 = (par + 1) % 2
                if isinstance(i, int) and i == -2:
                    pe.wait_ge(weights_in, 64)
                    pe.wait_ge(qkw_ready, 3)
                if isinstance(i, int) and i == 0:
                    pe.wait_ge(fcw_ready, 2)
                for s in range(SLOTS):
                    if within(m):
                        scores(i, par, s)
                    if s >= LAG:
                        if within(m):
                            weighted_sum(i, s - LAG)
                    elif within(o):
                        weighted_sum(i - 1, s - LAG + SLOTS)
                    if s == 0 and within(m):
                        if isinstance(m, int) and m < 2:
                            pe.wait_ge(qk_biased, m + 2)
                        else:
                            pe.wait_ge(out_added, m - 1)
                        for k in range(KH):
                            project(dense[:, P * k:P * (k + 1)], wv_sb, P * k, xT[:, par],
                                    v_ready if k == KH - 1 else None)
                    if s in (1, 2, 3, 4) and within(m):
                        if s == 1:
                            pe.wait_ge(v_biased, 2 * (m + 1))
                        if s == 3:
                            pe.wait_ge(u_ready, 2 * m + 1)
                        for f in (2 * s - 2, 2 * s - 1):
                            project(dense[:, P * (f % 4):P * (f % 4 + 1)], w1, P * f, hT[:, par],
                                    fc1_ready if f % 4 == 3 else None)
                    if s == 5 and within(n):
                        pe.wait_ge(norm_step, 6 * (n + 1))
                        if within(m):
                            pe.wait_ge(u_ready, 2 * m + 2)
                        else:
                            wait(pe, qk_biased, n)
                        for k, (src, c) in enumerate(((xn, 0), (xn, 1), (hn, 0), (hn, 1))):
                            last = nc.tensor.transpose(dense[:, P * k:P * (k + 1)], src[:, par, P * c:P * (c + 1)],
                                                       identity[:])
                        last.then_inc(transposed, 1)
                    if s in (7, 8) and within(n):
                        if s == 7:
                            pe.wait_ge(xT_copied, 3 * (n + 1))
                        w = (wq_sb, wk_sb)[s - 7]
                        for k in range(KH):
                            q = KH * (s - 7) + k
                            project(dense[:, P * q:P * (q + 1)], w, P * k, xT[:, par],
                                    qk_ready if q == 2 * KH - 1 else None)
                    if s in OUT_PRODUCTS and within(o):
                        if s == 9:
                            if within(n):
                                pe.wait_ge(qk_biased, n + 1)
                            elif within(m):
                                pe.wait_ge(u_ready, 2 * m + 2)
                            else:
                                pe.wait_ge(out_added, o)
                            pe.wait_ge(y_step, 4 * (o + 1))
                        for k in OUT_PRODUCTS[s]:
                            if k == FT:
                                pe.wait_ge(oT_ready, o + 1)
                            lhs, rhs = (yT[:, par1, k], w2[:, k]) if k < FT else (oT[:, par1, k - FT], wo_sb[:, k - FT])
                            last = nc.tensor.matmul(dense[:, 0:H], lhs, rhs, start=(k == 0), stop=(k == FT + KH - 1))
                        if s == 15:
                            last.then_inc(out_ready, 1)

            steps(pe, step)


def kernel(**inputs):
    import numpy as np
    import concourse.bacc as bacc
    from concourse.bass_utils import run_bass_kernel_spmd

    P = 128
    a = {k.replace("L0_", ""): np.ascontiguousarray(v) for k, v in inputs.items()}
    shape = a["attn_X_embed"].shape
    rows, hidden = shape[0] * shape[1], shape[2]

    def by_feature(v):
        return v.reshape(-1, P).T

    def stacking_order(v):
        w = v.reshape(v.shape[:-1] + (-1, P // 16, 16))
        return np.ascontiguousarray(np.swapaxes(w, -1, -2).reshape(v.shape))

    arrays = {
        "x": a["attn_X_embed"].reshape(rows, hidden),
        "wq": stacking_order(a["attn_Wq"]), "wk": stacking_order(a["attn_Wk"]), "wv": a["attn_Wv"], "wo": a["attn_Wo"],
        "feature_cols": np.ascontiguousarray(np.concatenate(
            [by_feature(v) for v in (stacking_order(a["attn_bq"]), stacking_order(a["attn_bk"]), a["attn_bv"],
                                     a["ffn_ln_gamma"], a["ffn_ln_beta"])], axis=1)),
        "fc1_bias_cols": np.ascontiguousarray(by_feature(a["ffn_fc1_bias"])),
        "bo": a["attn_bo"],
        "fc1_q": a["ffn_fc1_q"], "fc1_scales": a["ffn_fc1_scales"],
        "fc2_q": a["ffn_fc2_q"], "fc2_scales": a["ffn_fc2_scales"],
        "fc2_bias": a["ffn_fc2_bias"],
    }
    nc = bacc.Bacc("TRN2", target_bir_lowering=False, num_devices=1)
    args = {k: nc.dram_tensor(f"in_{k}", v.shape, mybir.dt.from_np(v.dtype), kind="ExternalInput").ap()
            for k, v in arrays.items()}
    out = nc.dram_tensor("out", (rows, hidden), mybir.dt.float32, kind="ExternalOutput").ap()
    attention_ffn_kernel(nc, **args, out=out)
    r = run_bass_kernel_spmd(nc, [{f"in_{k}": v for k, v in arrays.items()}], core_ids=[0])
    return r.results[0]["out"].reshape(shape)
```

```python
import concourse.bass as bass
from concourse import mybir
from contextlib import ExitStack


def attention_ffn_kernel(nc, x, wq, wk, wv, wo, feature_cols, fc1_bias_cols, bo, fc1_q, fc1_scales,
                         fc2_q, fc2_scales, fc2_bias, out):
    fp32 = mybir.dt.float32
    bf16 = mybir.dt.bfloat16
    i32 = mybir.dt.int32
    f32r = mybir.dt.float32r
    ALU = mybir.AluOpType
    ACT = mybir.ActivationFunctionType
    AXX = mybir.AxisListType.X

    P = 128
    ROWS, H = x.shape
    F = fc1_q.shape[1]
    TILES = ROWS // P
    DH = 16
    NJ = H // DH
    KH = H // P
    FT = F // P
    HR = 64
    HEADS = P // HR
    TOK = HR * NJ
    JH = P // DH
    KB = TOK // P
    SLOTS = HEADS * KB
    NSC = 3
    NE = 8
    LAG = 5
    QT = TOK // 4
    JQ = QT // HR
    SC = float(H) ** -0.5
    EPS = 1e-5
    PAIRS = (3, 2, 1)
    STACK = sum(PAIRS) * DH

    ctx = ExitStack()
    with ctx:
        def sb(name, shape, dt=fp32):
            return ctx.enter_context(nc.sbuf_tensor(name, shape, dt))

        def sem(name):
            return ctx.enter_context(nc.semaphore(name))

        identity = sb("identity", [P, P])
        wq_sb = sb("wq_sb", [P, KH, H])
        wk_sb = sb("wk_sb", [P, KH, H])
        wv_sb = sb("wv_sb", [P, KH, H])
        wo_sb = sb("wo_sb", [P, KH, H])
        cols = sb("cols", [P, 5, KH])
        bias_qk = sb("bias_qk", [P, 2 * HEADS * KH])
        b1 = sb("b1", [P, FT])
        bo_row = sb("bo_row", [P, H])
        b2_row = sb("b2_row", [P, H])
        w1 = sb("w1", [P, KH, F])
        w2 = sb("w2", [P, FT, H])
        w1h = sb("w1h", [P, KH, F], f32r)
        w1l = sb("w1l", [P, KH, F], f32r)
        w2h = sb("w2h", [P, FT, H], f32r)
        w2l = sb("w2l", [P, FT, H], f32r)
        woh = sb("woh", [P, KH, H], f32r)
        wol = sb("wol", [P, KH, H], f32r)
        xt = sb("xt", [P, 2, H])
        xn = sb("xn", [P, 2, H])
        hn = sb("hn", [P, 2, H])
        stats = sb("stats", [P, 2, 6])
        moments = sb("moments", [P, 2, 2])
        veps = sb("veps", [P, 2, 1])
        rstd = sb("rstd", [P, 2, 1])
        minus_half = sb("minus_half", [P, 1])
        warm = sb("warm", [P, 1])
        residual = sb("residual", [P, 2, H])
        base1 = sb("base1", [P, 2, H])
        base = sb("base", [P, 2, H])
        nT = sb("nT", [P, 2, 2 * KH, P])
        xT, hT = nT[:, :, 0:KH], nT[:, :, KH:2 * KH]
        hTh = sb("hTh", [P, 2, KH, P], f32r)
        hTl = sb("hTl", [P, 2, KH, P], f32r)
        qk32 = sb("qk32", [P, 2, 2, H])
        rest = sb("rest", [P, 2, 2, H])
        parts = sb("parts", [P, 2, 2, 3, H], bf16)
        qs = sb("qs", [STACK, 2, JH, HEADS, KH, HR], bf16)
        ks = sb("ks", [STACK, 2, JH, HEADS, KH * HR], bf16)
        nmax = sb("nmax", [P, NE, 1])
        zsum = sb("zsum", [P, NE, 1])
        rz = sb("rz", [P, NE, 32])
        ex = sb("ex", [P, NE, TOK])
        wrow = sb("wrow", [P, 2, QT])
        vT = sb("vT", [P, 2, KH, P])
        wT = sb("wT", [P, 2, KH, P])
        oT = sb("oT", [P, KH, P])
        oTh = sb("oTh", [P, KH, P], f32r)
        oTl = sb("oTl", [P, KH, P], f32r)
        u = sb("u", [P, 2, FT, P])
        th = sb("th", [P, 2, FT, P])
        yT = sb("yT", [P, 2, FT, P])
        yTh = sb("yTh", [P, 2, FT, P], f32r)
        yTl = sb("yTl", [P, 2, FT, P], f32r)
        res = sb("res", [P, 2, H])
        q1 = u[:].rearrange("p t f r -> p (t f r)").bitcast(i32).rearrange("p (k n) -> p k n", k=KH)
        s1 = th[:].rearrange("p t f r -> p (t f r)").rearrange("p (k n) -> p k n", k=KH)
        q2, s2 = (ex[:, a:a + 2].rearrange("p b t -> p (b t)").rearrange("p (k n) -> p k n", k=FT) for a in (0, 2))
        q2 = q2.bitcast(i32)

        score = [ctx.enter_context(nc.psum_tensor(f"score{b}", [P, TOK], fp32)) for b in range(NSC)]
        wacc = ctx.enter_context(nc.psum_tensor("wacc", [P, 512], fp32))
        dense = ctx.enter_context(nc.psum_tensor("dense", [P, 512], fp32))

        parts_d = nc.dram_tensor("parts_d", [2, 2, 3, P, H], bf16, kind="Internal").ap()
        w_d = nc.dram_tensor("w_d", [2, NJ, P], fp32, kind="Internal").ap()

        qkw_in, wv_in, wo_in = sem("qkw_in"), sem("wv_in"), sem("wo_in")
        cols_in = sem("cols_in")
        rows_in = sem("rows_in")
        fc1_in, fc2_in = sem("fc1_in"), sem("fc2_in")
        consts_ready = sem("consts_ready")
        identity_zeroed = sem("identity_zeroed")
        table_loaded = sem("table_loaded")
        qkw_ready = sem("qkw_ready")
        w1_ready = sem("w1_ready")
        beta_done = sem("beta_done")
        b1_ready = sem("b1_ready")
        w2_ready = sem("w2_ready")
        high_ready = sem("high_ready")
        low_ready = sem("low_ready")
        bias_ready = sem("bias_ready")
        x_loaded = [sem(f"x_loaded{k}") for k in range(2)]
        stats_step = sem("stats_step")
        norm_step = sem("norm_step")
        residual_ready = sem("residual_ready")
        base1_ready = sem("base1_ready")
        base_ready = sem("base_ready")
        transposed = sem("transposed")
        nT_copied = sem("nT_copied")
        qk_ready = sem("qk_ready")
        qk_biased = sem("qk_biased")
        cast_step = sem("cast_step")
        split_step = sem("split_step")
        parts_stored = sem("parts_stored")
        q_stacked = [sem(f"q_stacked{k}") for k in range(2)]
        k_stacked = [sem(f"k_stacked{k}") for k in range(2)]
        scores_ready = sem("scores_ready")
        max_ready = sem("max_ready")
        exp_done = sem("exp_done")
        rz_ready = sem("rz_ready")
        wsum_done = sem("wsum_done")
        w_copied = sem("w_copied")
        w_stored = [sem(f"w_stored{k}") for k in range(2)]
        w_spread = [sem(f"w_spread{k}") for k in range(2)]
        v_ready = sem("v_ready")
        v_biased = sem("v_biased")
        oT_ready = sem("oT_ready")
        oT_high = sem("oT_high")
        oT_low = sem("oT_low")
        yT_high = sem("yT_high")
        yT_low = sem("yT_low")
        hT_low = sem("hT_low")
        fc1_ready = sem("fc1_ready")
        u_ready = sem("u_ready")
        tanh_ready = sem("tanh_ready")
        y_step = sem("y_step")
        out_ready = sem("out_ready")
        out_added = sem("out_added")
        out_stored = [sem(f"out_stored{k}") for k in range(2)]

        block = ctx.enter_context(nc.Block())

        def within(t, lo=0, hi=TILES - 1):
            return not isinstance(t, int) or lo <= t <= hi

        def steps(engine, body):
            for i in range(-3, LOOP_START):
                body(i, i % 2)
            with engine.Fori(LOOP_START, LOOP_END - 1, 2) as i:
                body(i, 0)
                body(i + 1, 1)
            for i in range(LOOP_END, TILES + 1):
                body(i, i % 2)

        def wait(engine, sem_, value):
            if not isinstance(value, int) or value > 0:
                engine.wait_ge(sem_, value)

        def dma_count(t, par, dmas=1):
            return 8 * dmas * (t - par + 2)

        def wait_all(engine, *waits):
            waits = [(sem_, v) for sem_, v in waits if not isinstance(v, int) or v > 0]
            waits = [(sem_, v if isinstance(v, int) else engine.to_reg(v)) for sem_, v in waits]
            for sem_, v in waits:
                engine.wait_ge(sem_, v)

        def wait_apart(engine, *waits):
            wait_all(engine, (consts_ready, 1), *waits)

        def score_buf(par, s):
            return (SLOTS * par + s) % NSC

        def score_gap(par, s):
            n = SLOTS * par + s
            return NSC if n >= NSC or (2 * SLOTS) % NSC == 0 else (2 * SLOTS) % NSC

        def ebuf(s):
            return s % NE

        LOOP_START = 4
        LOOP_END = TILES - 4
        STATS_SLOTS = (0, 1, 2, 10, 11, 12)
        V_SLOT = (0, 0)
        T_SLOT = (6, 2)
        QK_SLOT = (8, 4)
        FC1_SLOTS = ({2: 2, 4: 3}, {6: 0, 8: 1})
        OUT_PRODUCTS = {10: (0, 1, 2), 12: (3, 4, 5), 14: (6, 7, 8, 9)}
        CAST_SLOTS = ((10, 12), (6, 8))
        TANH_SLOTS = ({4: 2, 7: 3}, {8: 0, 10: 1})
        Y_CAST_SLOT = (12, 2)
        ORDER = (("v", 2, 3, "t", "qk", "out"), ("v", "t", "qk", 0, 1, "out"))

        def pair(i, par):
            return i + par

        def quarter(q):
            return slice(q * FT // 4, (q + 1) * FT // 4)

        def group(i, par, g):
            if g == "v":
                return within(i), v_biased, 2 * (i + 1)
            if g == "t":
                return within(i + 2), nT_copied, 2 * (i + 3)
            if g == "qk":
                return within(i + 2), qk_biased, i + 3
            if g == "out":
                return within(i - 1), out_added, i
            return within(pair(i, par)), u_ready, 2 * pair(i, par) + g + 1

        def wait_bank(engine, i, par, g):
            at = ORDER[par].index(g)
            before = [(i, par, b) for b in ORDER[par][:at]]
            before = [(i - 1, 1 - par, b) for b in ORDER[1 - par]] + before
            for b in reversed(before):
                exists, sem_, count = group(*b)
                if exists:
                    wait(engine, sem_, count)
                    return

        @block.sync
        def _(sp):
            def load_x(t, par):
                row = t * P if isinstance(t, int) else sp.snap(t * P)
                wait(sp, residual_ready, t - 1)
                sp.dma_start(xt[:, par, :], x[bass.ds(row, P), :]).then_inc(x_loaded[par], 16)

            load_x(0, 0)
            sp.dma_start(wq_sb[:], wq.rearrange("(k p) n -> p k n", p=P)).then_inc(qkw_in, 16)
            sp.dma_start(wk_sb[:], wk.rearrange("(k p) n -> p k n", p=P)).then_inc(qkw_in, 16)
            sp.dma_start(cols[:], feature_cols.rearrange("p (c k) -> p c k", k=KH)).then_inc(cols_in, 16)
            load_x(1, 1)
            sp.dma_start(q1, fc1_q.rearrange("(k p) n -> p k n", p=P)).then_inc(fc1_in, 16)
            sp.dma_start(s1, fc1_scales.partition_broadcast(P)).then_inc(fc1_in, 16)
            sp.dma_start(b1[:], fc1_bias_cols).then_inc(rows_in, 16)
            sp.dma_start(bo_row[:], bo.partition_broadcast(P)).then_inc(rows_in, 16)
            sp.dma_start(b2_row[:], fc2_bias.partition_broadcast(P)).then_inc(rows_in, 16)
            sp.dma_start(wv_sb[:], wv.rearrange("(k p) n -> p k n", p=P)).then_inc(wv_in, 16)
            sp.dma_start(q2, fc2_q.rearrange("(k p) n -> p k n", p=P)).then_inc(fc2_in, 16)
            sp.dma_start(s2, fc2_scales.partition_broadcast(P)).then_inc(fc2_in, 16)
            sp.dma_start(wo_sb[:], wo.rearrange("(k p) n -> p k n", p=P)).then_inc(wo_in, 16)

            def store_w(t, par, head):
                h = HEADS * t + head
                wait_all(sp, (w_copied, h + 1), (w_spread[par], dma_count(t - 2, par, KH)))
                sp.dma_start(w_d[par, :, head * HR:(head + 1) * HR].rearrange("(c j) r -> c j r", c=4),
                             wrow[0:97:32, head, :].rearrange("c (j r) -> c j r", j=JQ)).then_inc(w_stored[head], 16)

            def step(i, par):
                n, k, m, o = i + 2, i + 1, i, i - 1
                kpar = opar = (par + 1) % 2
                if within(i, -2) and within(i + 4):
                    load_x(i + 4, par)
                if within(k):
                    wait_all(sp, (parts_stored, 16 * (k + 1)), (scores_ready, SLOTS * (k - 1)))
                    qd, kd = (parts_d[kpar, which].rearrange("a (c j) t -> (a c) (j t)", c=DH) for which in (0, 1))
                    for a, met in enumerate(PAIRS):
                        at = DH * sum(PAIRS[:a])
                        part_a = qd[DH * a:DH * (a + 1)].unsqueeze(0).to_broadcast([met, DH, JH * H])
                        sp.dma_start(ks[at:at + DH * met, kpar], kd[0:DH * met]).then_inc(k_stacked[kpar], 16)
                        sp.dma_start(qs[at:at + DH * met, kpar], part_a).then_inc(q_stacked[kpar], 16)
                if within(o):
                    store_w(o, opar, 1)
                    wait_all(sp, (w_stored[0], 16 * (o + 1)), (w_stored[1], 16 * (o + 1)), (oT_ready, o - 1))
                    for h in range(KH):
                        src = w_d[opar, 8 * h:8 * h + 8, :].unsqueeze(1).to_broadcast([8, DH, P])
                        sp.dma_start(wT[:, opar, h, :], src).then_inc(w_spread[opar], 16)
                if within(m):
                    store_w(m, par, 0)
                if within(n):
                    wait_all(sp, (cast_step, 2 * (n + 1)), (split_step, 2 * (n + 1)), (q_stacked[par], dma_count(n - 2, par, len(PAIRS))),
                             (k_stacked[par], dma_count(n - 2, par, len(PAIRS))))
                    sp.dma_start(parts_d[par].rearrange("w a p t -> p (w a) t"),
                                 parts[:, par].rearrange("p w a t -> p (w a) t")).then_inc(parts_stored, 16)
                if within(o):
                    row = o * P if isinstance(o, int) else sp.snap(o * P)
                    sp.wait_ge(out_added, o + 1)
                    sp.dma_start(out[bass.ds(row, P), :], res[:, opar, :]).then_inc(out_stored[opar], 16)

            steps(sp, step)
            for par in range(2):
                sp.wait_ge(out_stored[par], dma_count(TILES - 2 + par, par))

        @block.gpsimd
        def _(pool):
            nc.gpsimd.memset(identity[:], 0.0).then_inc(identity_zeroed, 1)
            pool.wait_ge(identity_zeroed, 1)
            nc.gpsimd.affine_select(out=identity[:], in_=identity[:], compare_op=ALU.not_equal, fill=1.0,
                                    base=0, pattern=[[-1, P]], channel_multiplier=1).then_inc(consts_ready, 1)
            nc.gpsimd.memset(rz[:], 0.0).then_inc(consts_ready, 1)
            nc.gpsimd.memset(minus_half[:], -0.5).then_inc(identity_zeroed, 1)
            pool.wait_ge(identity_zeroed, 2)

            def normalise(t, par, which):
                src, dst = ((xt, xn), (xn, hn))[which]
                pool.wait_ge(stats_step, 6 * t + 3 * which + 3)
                nc.gpsimd.tensor_tensor(rstd[:, which], veps[:, which], minus_half[:], ALU.pow).then_inc(norm_step, 1)
                last_read = ((transposed, t - 1), (residual_ready, t - 1)) if which == 0 else ((transposed, t - 1),)
                for sem_, count in last_read:
                    wait(pool, sem_, count)
                nc.gpsimd.tensor_tensor(dst[:, par], src[:, par], moments[:, which, 0:1].to_broadcast([P, H]),
                                        ALU.subtract).then_inc(norm_step, 1)
                pool.wait_ge(norm_step, 6 * t + 3 * which + 2)
                nc.gpsimd.tensor_tensor(dst[:, par], dst[:, par], rstd[:, which].to_broadcast([P, H]),
                                        ALU.mult).then_inc(norm_step, 1)

            def silu(i, par, q):
                p0, f = pair(i, par), quarter(q)
                pool.wait_ge(tanh_ready, 2 * p0 + q + 1)
                nc.gpsimd.tensor_tensor(th[:, :, f], th[:, :, f], u[:, :, f], ALU.mult).then_inc(y_step, 1)
                pool.wait_ge(y_step, 4 * p0 + 2 * q + 1)
                wait(pool, yT_low, p0)
                wait(pool, yT_high, p0)
                nc.gpsimd.tensor_tensor(yT[:, :, f], th[:, :, f], u[:, :, f], ALU.add).then_inc(y_step, 1)

            def y_low(t, par):
                pool.wait_ge(yT_high, t + 1)
                wait(pool, out_ready, t - 1)
                nc.gpsimd.tensor_tensor(yTl[:, par], yT[:, par], yTh[:, par].bitcast(fp32),
                                        ALU.subtract).then_inc(yT_low, 1)

            def h_low(t, par):
                pool.wait_ge(nT_copied, 2 * (t + 1))
                nc.gpsimd.tensor_tensor(hTl[:, par], hT[:, par], hTh[:, par].bitcast(fp32),
                                        ALU.subtract).then_inc(hT_low, 1)

            def step(i, par):
                l, n, k, m, o = i + 3, i + 2, i + 1, i, i - 1
                par1 = (par + 1) % 2
                p0 = pair(i, par)
                if within(m):
                    pool.wait_ge(base1_ready, m + 1)
                    wait(pool, out_added, m - 1)
                    nc.gpsimd.tensor_tensor(base[:, par], base1[:, par], b2_row[:], ALU.add).then_inc(base_ready, 1)
                if within(k):
                    if isinstance(k, int) and k == 0:
                        pool.wait_ge(bias_ready, 1)
                    pool.wait_ge(residual_ready, k + 1)
                    wait(pool, base_ready, k - 1)
                    nc.gpsimd.tensor_tensor(base1[:, par1], residual[:, par1], bo_row[:],
                                            ALU.add).then_inc(base1_ready, 1)
                if par == 1 and within(o):
                    y_low(o, 0)
                if within(l):
                    normalise(l, par1, 0)
                if par == 1 and within(n):
                    h_low(n, par)
                if par == 1 and within(m):
                    y_low(m, 1)
                if par == 0 and within(p0):
                    silu(i, par, 2)
                if within(l):
                    pool.wait_ge(norm_step, 6 * l + 3)
                    wait(pool, base1_ready, l - 1)
                    nc.gpsimd.tensor_tensor(residual[:, par1], xt[:, par1], xn[:, par1],
                                            ALU.add).then_inc(residual_ready, 1)
                if par == 0 and within(p0):
                    silu(i, par, 3)
                if par == 0 and within(n):
                    h_low(n, par)
                if par == 1 and within(n):
                    rest_of_parts(n, par)
                if within(o):
                    pool.wait_ge(w_spread[par1], dma_count(o, par1, KH))
                    pool.wait_ge(v_biased, 2 * (o + 1))
                    wait(pool, oT_low, o)
                    wait(pool, oT_high, o)
                    nc.gpsimd.tensor_tensor(oT[:], vT[:, par1], wT[:, par1], ALU.mult).then_inc(oT_ready, 1)
                if par == 0 and within(n):
                    rest_of_parts(n, par)
                if par == 1 and within(p0):
                    silu(i, par, 0)
                if within(o):
                    pool.wait_ge(oT_high, o + 1)
                    wait(pool, out_ready, o)
                    nc.gpsimd.tensor_tensor(oTl[:], oT[:], oTh[:].bitcast(fp32), ALU.subtract).then_inc(oT_low, 1)
                if within(n):
                    pool.wait_ge(cast_step, 2 * n + 2)
                    wait(pool, parts_stored, 16 * (n - 1))
                    nc.gpsimd.tensor_tensor(parts[:, par, :, 2], rest[:, par], parts[:, par, :, 1],
                                            ALU.subtract).then_inc(split_step, 1)
                if par == 1 and within(p0):
                    silu(i, par, 1)
                if within(l):
                    normalise(l, par1, 1)

            def rest_of_parts(n, par):
                pool.wait_ge(cast_step, 2 * n + 1)
                nc.gpsimd.tensor_tensor(rest[:, par], qk32[:, par], parts[:, par, :, 0],
                                        ALU.subtract).then_inc(split_step, 1)

            steps(pool, step)

        @block.scalar
        def _(act):
            act.wait_ge(identity_zeroed, 2)
            nc.scalar.activation(warm[:], minus_half[:], ACT.Exp).then_inc(table_loaded, 1)
            act.wait_ge(cols_in, 16)

            def copy_w(t, head):
                h = HEADS * t + head
                act.wait_ge(wsum_done, KB * (h + 1))
                wait(act, w_stored[head], 16 * t)
                nc.scalar.activation(wrow[:, head], wacc[:, 0:QT], ACT.Copy).then_inc(w_copied, 1)

            def high_w1():
                act.wait_ge(w1_ready, 1)
                for k in range(KH):
                    nc.scalar.activation(w1h[:, k], w1[:, k], ACT.Copy, scale=cols[:, 3, k:k + 1]).then_inc(high_ready, 1)

            def high_w2_wo():
                act.wait_ge(w2_ready, 1)
                nc.scalar.activation(w2h[:], w2[:], ACT.Copy, scale=0.25).then_inc(high_ready, 1)
                act.wait_ge(wo_in, 16)
                nc.scalar.activation(woh[:], wo_sb[:], ACT.Copy).then_inc(high_ready, 1)

            def step(i, par):
                n, m, o = i + 2, i, i - 1
                par1 = (par + 1) % 2
                for s in range(SLOTS):
                    if s == 0 and isinstance(i, int) and i == -1:
                        high_w1()
                    if s == 8 and isinstance(i, int) and i == -1:
                        high_w2_wo()
                    if s == 0 and within(m):
                        act.wait_ge(v_ready, m + 1)
                        wait(act, oT_ready, m - 1)
                        for k in range(KH):
                            nc.scalar.activation(vT[:, par, k], dense[:, k * P:(k + 1) * P], ACT.Identity,
                                                 bias=cols[:, 2, k:k + 1]).then_inc(v_biased, 1)
                    if s == T_SLOT[par] and within(n):
                        act.wait_ge(transposed, n + 1)
                        wait(act, hT_low, n - 1)
                        nc.scalar.activation(nT[:, par], dense[:].rearrange("p (k r) -> p k r", k=2 * KH),
                                             ACT.Copy).then_inc(nT_copied, 1)
                        nc.scalar.activation(hTh[:, par], dense[:, KH * P:].rearrange("p (k r) -> p k r", k=KH),
                                             ACT.Copy).then_inc(nT_copied, 1)
                    if s == 3 and within(o):
                        copy_w(o, 1)
                    if s == 11 and within(m):
                        copy_w(m, 0)
                    if within(m):
                        g = SLOTS * i + s
                        act.wait_ge(max_ready, g + 1)
                        wait(act, wsum_done, g - NE + 1)
                        nc.scalar.activation(ex[:, ebuf(s)], score[score_buf(par, s)][:], ACT.Exp,
                                             bias=nmax[:, ebuf(s)], accum_out=zsum[:, ebuf(s)]).then_inc(exp_done, 1)
                    if s in CAST_SLOTS[par] and within(n):
                        c = CAST_SLOTS[par].index(s)
                        src, ready, count = ((qk32, qk_biased, n + 1), (rest, split_step, 2 * n + 1))[c]
                        act.wait_ge(ready, count)
                        wait(act, parts_stored, 16 * (n - 1))
                        nc.scalar.activation(parts[:, par, :, c], src[:, par],
                                             ACT.Copy).then_inc(cast_step, 1)
                    if s in TANH_SLOTS[par] and within(pair(i, par)):
                        q, p0 = TANH_SLOTS[par][s], pair(i, par)
                        act.wait_ge(u_ready, 2 * p0 + q + 1)
                        wait(act, y_step, 4 * (p0 - 2) + 2 * q + 2)
                        nc.scalar.activation(th[:, :, quarter(q)], u[:, :, quarter(q)], ACT.Tanh,
                                             scale=0.5).then_inc(tanh_ready, 1)

            steps(act, step)

        @block.vector
        def _(dve):
            def scale_qk():
                dve.wait_ge(qkw_in, 32)
                dve.wait_ge(cols_in, 16)
                nc.vector.tensor_scalar(wq_sb[:], wq_sb[:], SC, None, ALU.mult).then_inc(qkw_ready, 1)
                nc.vector.tensor_scalar(wk_sb[:], wk_sb[:], SC, None, ALU.mult).then_inc(qkw_ready, 1)
                nc.vector.tensor_scalar(bias_qk[:].rearrange("p (w h k) -> p w h k", w=2, h=HEADS),
                                        cols[:, 0:2].unsqueeze(2).to_broadcast([P, 2, HEADS, KH]),
                                        SC, None, ALU.mult).then_inc(qkw_ready, 1)
            def dequantise_fc1():
                dve.wait_ge(fc1_in, 32)
                nc.vector.scalar_tensor_tensor(w1[:], q1, -128.0, s1, ALU.add, ALU.mult).then_inc(w1_ready, 1)
                dve.wait_ge(rows_in, 48)
                nc.vector.tensor_scalar(b2_row[:], b2_row[:], 0.5, None, ALU.mult).then_inc(bias_ready, 1)

            def low_w1():
                dve.wait_ge(high_ready, KH)
                for k in range(KH):
                    nc.vector.scalar_tensor_tensor(w1l[:, k], w1[:, k], cols[:, 3, k:k + 1], w1h[:, k].bitcast(fp32),
                                                   ALU.mult, ALU.subtract).then_inc(low_ready, 1)
                dve.wait_ge(beta_done, 1)
                nc.vector.tensor_tensor(b1[:], b1[:], wacc[:, 0:FT], ALU.add).then_inc(b1_ready, 1)
                dve.wait_ge(b1_ready, 1)

            def dequantise_fc2():
                dve.wait_ge(fc2_in, 32)
                nc.vector.scalar_tensor_tensor(w2[:], q2, -128.0, s2, ALU.add, ALU.mult).then_inc(w2_ready, 1)

            def low_w2_wo():
                dve.wait_ge(high_ready, KH + 1)
                nc.vector.scalar_tensor_tensor(w2l[:], w2[:], 0.25, w2h[:].bitcast(fp32), ALU.mult,
                                               ALU.subtract).then_inc(low_ready, 1)
                dve.wait_ge(high_ready, KH + 2)
                nc.vector.tensor_tensor(wol[:], wo_sb[:], woh[:].bitcast(fp32), ALU.subtract).then_inc(low_ready, 1)

            def statistics(t, par, k):
                which = k // 3
                if k == 0:
                    dve.wait_ge(x_loaded[par], dma_count(t, par))
                elif k == 3:
                    dve.wait_ge(norm_step, 6 * t + 3)
                else:
                    (wait_apart if k % 3 == 1 else wait_all)(dve, (stats_step, 6 * t + k))
                if k % 3 == 0:
                    ins = nc.vector.bn_stats(stats[:, which], (xt, xn)[which][:, par])
                elif k % 3 == 1:
                    ins = nc.vector.bn_aggr(moments[:, which], stats[:, which])
                else:
                    ins = nc.vector.tensor_scalar(veps[:, which], moments[:, which, 1:2], EPS, None, ALU.add)
                ins.then_inc(stats_step, 1)

            def reciprocals(g, s):
                dve.wait_ge(exp_done, g + 2)
                if isinstance(g, int) and g == 0:
                    dve.wait_ge(consts_ready, 2)
                e = ebuf(s)
                nc.vector.reciprocal(rz[:, e:e + 2, 0:1], zsum[:, e:e + 2]).then_inc(rz_ready, 1)

            def step(i, par):
                l, n, m, o = i + 3, i + 2, i, i - 1
                par1 = (par + 1) % 2
                if isinstance(i, int) and i == -2:
                    scale_qk()
                for s in range(SLOTS):
                    if s - 1 in FC1_SLOTS[par] and within(pair(i, par)):
                        q, p0 = FC1_SLOTS[par][s - 1], pair(i, par)
                        dve.wait_ge(fc1_ready, 2 * p0 + q + 1)
                        wait(dve, y_step, 4 * (p0 - 2) + 2 * q + 2)
                        nc.vector.tensor_tensor(u[:, :, quarter(q)],
                                                dense[:].rearrange("p (f t r) -> p t f r", f=FT // 4, t=2),
                                                b1[:, quarter(q)].unsqueeze(1).unsqueeze(3).to_broadcast([P, 2, FT // 4, P]),
                                                ALU.add).then_inc(u_ready, 1)
                    if s == 9 and isinstance(i, int) and i == -2:
                        dequantise_fc1()
                    if s == 6 and isinstance(i, int) and i == 0:
                        low_w2_wo()
                    if isinstance(i, int) and i == -1:
                        if s == 2:
                            low_w1()
                        if s == 4:
                            dequantise_fc2()
                    if s - 1 == QK_SLOT[par] and within(n):
                        dve.wait_ge(qk_ready, n + 1)
                        wait(dve, split_step, 2 * (n - 1))
                        nc.vector.tensor_tensor(qk32[:, par].rearrange("p w (b r) -> p (w b) r", r=HR),
                                                dense[:].rearrange("p (b r) -> p b r", r=HR),
                                                bias_qk[:].unsqueeze(2).to_broadcast([P, 2 * HEADS * KH, HR]),
                                                ALU.add).then_inc(qk_biased, 1)
                    if s == 15 and within(o):
                        dve.wait_ge(out_ready, o + 1)
                        dve.wait_ge(base_ready, o + 1)
                        wait(dve, out_stored[par1], dma_count(o - 2, par1))
                        nc.vector.tensor_tensor(res[:, par1], dense[:, 0:H], base[:, par1], ALU.add).then_inc(out_added, 1)
                    if within(m):
                        g = SLOTS * i + s
                        dve.wait_ge(scores_ready, g + 1)
                        nc.vector.tensor_reduce(nmax[:, ebuf(s)], score[score_buf(par, s)][:], AXX, ALU.max,
                                                negate=True).then_inc(max_ready, 1)
                    if s % 2 and within(SLOTS * i + s - 3, 0, SLOTS * TILES - 1):
                        reciprocals(SLOTS * i + s - 3, (s - 3) % SLOTS)
                    if s == Y_CAST_SLOT[par] and within(m):
                        dve.wait_ge(y_step, 4 * (m - par) + 8)
                        wait(dve, out_ready, m - 1)
                        nc.vector.tensor_copy(yTh[:, par], yT[:, par]).then_inc(yT_high, 1)
                    if s == 12 and within(o):
                        dve.wait_ge(oT_ready, o + 1)
                        wait(dve, out_ready, o)
                        nc.vector.tensor_copy(oTh[:], oT[:]).then_inc(oT_high, 1)
                    if s in STATS_SLOTS and within(l):
                        statistics(l, par1, STATS_SLOTS.index(s))

            steps(dve, step)

        @block.tensor
        def _(pe):
            pe.wait_ge(consts_ready, 2)

            def scores(i, par, s):
                g = SLOTS * i + s
                head, b = divmod(s, KB)
                if s == 0:
                    pe.wait_ge(q_stacked[par], dma_count(i, par, len(PAIRS)))
                    pe.wait_ge(k_stacked[par], dma_count(i, par, len(PAIRS)))
                wait(pe, exp_done, g - score_gap(par, s) + 1)
                for a in range(KH):
                    last = nc.tensor.matmul(score[score_buf(par, s)][:, 512 * a:512 * (a + 1)],
                                            ks[:, par, b, head], qs[:, par, :, head, a],
                                            start=True, stop=True)
                last.then_inc(scores_ready, 1)

            def weighted_sum(i, s):
                g = SLOTS * i + s
                head, b = divmod(s, KB)
                if s % 2 == 0:
                    pe.wait_ge(rz_ready, (SLOTS // 2) * i + s // 2 + 1)
                if b == 0:
                    wait(pe, w_copied, HEADS * i + head)
                for c in range(4):
                    last = nc.tensor.matmul(wacc[32 * c:32 * c + 32, 0:QT], rz[:, ebuf(s)],
                                            ex[:, ebuf(s), QT * c:QT * (c + 1)],
                                            start=(b == 0), stop=(b == KB - 1), tile_position=(0, 32 * c))
                if s % 2:
                    last.then_inc(wsum_done, 2)

            def project(dst, w, k0, src, last_sem=None):
                for k in range(KH):
                    last = nc.tensor.matmul(dst, w[:, k, k0:k0 + P], src[:, k], start=(k == 0), stop=(k == KH - 1))
                if last_sem is not None:
                    last.then_inc(last_sem, 1)

            def step(i, par):
                n, m, o = i + 2, i, i - 1
                par1 = (par + 1) % 2
                if isinstance(i, int) and i == -2:
                    pe.wait_ge(qkw_ready, 3)
                if isinstance(i, int) and i == 1:
                    pe.wait_ge(low_ready, KH + 2)
                for s in range(SLOTS):
                    if within(m):
                        scores(i, par, s)
                    if s % 2:
                        for t in (s - LAG, s - LAG + 1):
                            if t >= 0 and within(m):
                                weighted_sum(i, t)
                            elif t < 0 and within(o):
                                weighted_sum(i - 1, t + SLOTS)
                    if s == V_SLOT[par] and within(m):
                        wait_bank(pe, i, par, "v")
                        if isinstance(m, int) and m == 0:
                            pe.wait_ge(wv_in, 16)
                        for k in range(KH):
                            project(dense[:, P * k:P * (k + 1)], wv_sb, P * k, xT[:, par],
                                    v_ready if k == KH - 1 else None)
                    if s in FC1_SLOTS[par] and within(pair(i, par)):
                        q = FC1_SLOTS[par][s]
                        if isinstance(i, int) and i == -1:
                            pe.wait_ge(low_ready, KH)
                            pe.wait_ge(b1_ready, 1)
                        wait_bank(pe, i, par, q)
                        pe.wait_ge(hT_low, pair(i, par) + 2)
                        for f in range(FT // 4):
                            at = P * (q * FT // 4 + f)
                            for k in range(KH):
                                wh, wl, hh, hl = w1h[:, k, at:at + P], w1l[:, k, at:at + P], hTh[:, :, k], hTl[:, :, k]
                                for c, (lhs, rhs) in enumerate(((wh, hh), (wh, hl), (wl, hh))):
                                    last = nc.tensor.matmul(dense[:, 2 * P * f:2 * P * (f + 1)], lhs, rhs,
                                                            start=(k == 0 and c == 0), stop=(k == KH - 1 and c == 2))
                        last.then_inc(fc1_ready, 1)
                    if s == T_SLOT[par] and within(n):
                        pe.wait_ge(norm_step, 6 * (n + 1))
                        wait_bank(pe, i, par, "t")
                        for k, (src, c) in enumerate(((xn, 0), (xn, 1), (hn, 0), (hn, 1))):
                            last = nc.tensor.transpose(dense[:, P * k:P * (k + 1)], src[:, par, P * c:P * (c + 1)],
                                                       identity[:])
                        last.then_inc(transposed, 1)
                    if s == QK_SLOT[par] and within(n):
                        wait_bank(pe, i, par, "qk")
                        for q in range(2 * KH):
                            w, k = divmod(q, KH)
                            dst = dense[:].rearrange("p (w h k r) -> p w h k r", w=2, h=HEADS, k=KH)[:, w, :, k]
                            project(dst, (wq_sb, wk_sb)[w], P * k, xT[:, par],
                                    qk_ready if q == 2 * KH - 1 else None)
                    if s in OUT_PRODUCTS and within(o):
                        if s == 10:
                            wait_bank(pe, i, par, "out")
                            pe.wait_ge(yT_low, o + 1)
                        for k in OUT_PRODUCTS[s]:
                            if k == FT:
                                pe.wait_ge(oT_low, o + 1)
                            ah, al, bh, bl = ((yTh[:, par1, k], yTl[:, par1, k], w2h[:, k], w2l[:, k]) if k < FT else
                                              (oTh[:, k - FT], oTl[:, k - FT], woh[:, k - FT], wol[:, k - FT]))
                            for c, (lhs, rhs) in enumerate(((ah, bh), (ah, bl), (al, bh))):
                                last = nc.tensor.matmul(dense[:, 0:H], lhs, rhs, start=(k == 0 and c == 0),
                                                        stop=(k == FT + KH - 1 and c == 2))
                        if s == 14:
                            last.then_inc(out_ready, 1)
                if isinstance(i, int) and i == -2:
                    pe.wait_ge(w1_ready, 1)
                    for f in range(FT):
                        project(wacc[:, f:f + 1], w1, P * f, cols[:, 4].unsqueeze(2), beta_done if f == FT - 1 else None)

            steps(pe, step)


def kernel(**inputs):
    import numpy as np
    import concourse.bacc as bacc
    from concourse.bass_utils import run_bass_kernel_spmd

    P = 128
    a = {k.replace("L0_", ""): np.ascontiguousarray(v) for k, v in inputs.items()}
    shape = a["attn_X_embed"].shape
    rows, hidden = shape[0] * shape[1], shape[2]

    def by_feature(v):
        return v.reshape(-1, P).T

    def stacking_order(v):
        w = v.reshape(v.shape[:-1] + (-1, P // 16, 16))
        return np.ascontiguousarray(np.swapaxes(w, -1, -2).reshape(v.shape))

    arrays = {
        "x": a["attn_X_embed"].reshape(rows, hidden),
        "wq": stacking_order(a["attn_Wq"]), "wk": stacking_order(a["attn_Wk"]), "wv": a["attn_Wv"], "wo": a["attn_Wo"],
        "feature_cols": np.ascontiguousarray(np.concatenate(
            [by_feature(v) for v in (stacking_order(a["attn_bq"]), stacking_order(a["attn_bk"]), a["attn_bv"],
                                     a["ffn_ln_gamma"], a["ffn_ln_beta"])], axis=1)),
        "fc1_bias_cols": np.ascontiguousarray(by_feature(a["ffn_fc1_bias"])),
        "bo": a["attn_bo"],
        "fc1_q": a["ffn_fc1_q"], "fc1_scales": a["ffn_fc1_scales"],
        "fc2_q": a["ffn_fc2_q"], "fc2_scales": a["ffn_fc2_scales"],
        "fc2_bias": a["ffn_fc2_bias"],
    }
    nc = bacc.Bacc("TRN2", target_bir_lowering=False, num_devices=1)
    args = {k: nc.dram_tensor(f"in_{k}", v.shape, mybir.dt.from_np(v.dtype), kind="ExternalInput").ap()
            for k, v in arrays.items()}
    out = nc.dram_tensor("out", (rows, hidden), mybir.dt.float32, kind="ExternalOutput").ap()
    attention_ffn_kernel(nc, **args, out=out)
    r = run_bass_kernel_spmd(nc, [{f"in_{k}": v for k, v in arrays.items()}], core_ids=[0])
    return r.results[0]["out"].reshape(shape)
```
